# Optimizing a Trainium2 kernel written in Bass

```python
import numpy as np
import jax
import jax.numpy as jnp

def _softmax(x, axis=-1):
    return jax.nn.softmax(x, axis=axis)

def _gelu(x):
    return jax.nn.gelu(x, approximate=True)

def _silu(x):
    return jax.nn.silu(x)

def _sigmoid(x):
    return jax.nn.sigmoid(x)

def _layernorm(x, axis=-1, eps=1e-05):
    m = jnp.mean(x, axis=axis, keepdims=True)
    v = jnp.var(x, axis=axis, keepdims=True)
    return (x - m) / jnp.sqrt(v + eps)

def _scatter_add(tgt, idx, src, axis=0):
    return tgt.at[idx].add(src)

def _segment_sum(src, seg, n):
    return jax.ops.segment_sum(src, seg, n)
kernel_name = 'mk_gnn_resnorm_d1_gnn_r64_87f48b'

def setup_inputs(seed: int=0):
    np.random.seed(seed)
    _w = jnp.asarray

    def _rec_inputs():
        import jax
        import jax.numpy as jnp
        _gk = jax.random.key(seed)
        x = -0.0003713 + 1 * jax.random.normal(jax.random.fold_in(_gk, 1), (50000, 256), jnp.float32)
        src = jax.random.randint(jax.random.fold_in(_gk, 2), (25000,), 0, 50000, jnp.int32)
        dst = jnp.minimum((50000 * jax.random.uniform(jax.random.fold_in(_gk, 3), (25000,)) ** 2.0).astype(jnp.int32), 49999)
        _o = jnp.argsort(dst, stable=True)
        src = src[_o]
        dst = dst[_o]
        return (x, src, dst)
    x, src, dst = _rec_inputs()

    def _L0_gnn_setup():
        import jax, jax.numpy as jnp
        import numpy as np
        N_NODES = 50000
        N_EDGES = 12500
        IN_CH = 256
        HID_CH = 256
        OUT_CH = 256
        N_LAYERS = 3
        key = jax.random.key(seed)
        ks = jax.random.split(key, 8)
        s_in = 1.0 / np.sqrt(IN_CH)
        s_h = 1.0 / np.sqrt(HID_CH)
        return {'x': jax.random.normal(ks[0], (N_NODES, IN_CH), dtype=jnp.float32), 'W_in': jax.random.normal(ks[1], (IN_CH, HID_CH), dtype=jnp.float32) * s_in, 'b_in': jnp.zeros((HID_CH,), dtype=jnp.float32), 'W_agg': jax.random.normal(ks[2], (N_LAYERS, HID_CH, HID_CH), dtype=jnp.float32) * s_h, 'W_self': jax.random.normal(ks[3], (N_LAYERS, HID_CH, HID_CH), dtype=jnp.float32) * s_h, 'b_hid': jnp.zeros((N_LAYERS, HID_CH), dtype=jnp.float32), 'W_out': jax.random.normal(ks[4], (HID_CH, OUT_CH), dtype=jnp.float32) * s_h, 'b_out': jnp.zeros((OUT_CH,), dtype=jnp.float32), 'edge_index': jax.random.randint(ks[5], (2, N_EDGES), 0, N_NODES, dtype=jnp.int64)}
    _L0_gnn_all = _L0_gnn_setup()
    _L0_gnn_in = {k: v for k, v in _L0_gnn_all.items() if k in ('W_in', 'b_in', 'W_agg', 'W_self', 'b_hid', 'W_out', 'b_out')}
    del _L0_gnn_all
    return {'x': x, 'src': src, 'dst': dst, 'L0_gnn_W_in': _L0_gnn_in['W_in'], 'L0_gnn_b_in': _L0_gnn_in['b_in'], 'L0_gnn_W_agg': _L0_gnn_in['W_agg'], 'L0_gnn_W_self': _L0_gnn_in['W_self'], 'L0_gnn_b_hid': _L0_gnn_in['b_hid'], 'L0_gnn_W_out': _L0_gnn_in['W_out'], 'L0_gnn_b_out': _L0_gnn_in['b_out']}

def reference(x, src, dst, L0_gnn_W_in, L0_gnn_b_in, L0_gnn_W_agg, L0_gnn_W_self, L0_gnn_b_hid, L0_gnn_W_out, L0_gnn_b_out):
    import jax
    import jax.numpy as jnp

    def _L0_gnn_ref(x, W_in, b_in, W_agg, W_self, b_hid, W_out, b_out, edge_index):
        import jax, jax.numpy as jnp
        import numpy as np
        N_NODES = 50000
        N_EDGES = 12500
        IN_CH = 256
        HID_CH = 256
        OUT_CH = 256
        N_LAYERS = 3
        n = x.shape[0]
        dst = edge_index[0]
        src = edge_index[1]
        n_layers = W_agg.shape[0]
        h = x @ W_in + b_in
        deg = jax.ops.segment_sum(jnp.ones_like(dst, dtype=h.dtype), dst, num_segments=n)
        deg = jnp.maximum(deg, 1.0)[:, None]
        for l in range(n_layers):
            agg = jax.ops.segment_sum(h[src], dst, num_segments=n) / deg
            h = jax.nn.relu(agg @ W_agg[l] + h @ W_self[l] + b_hid[l])
        return h @ W_out + b_out
    edge_index = jnp.stack([src, dst])
    x = _layernorm(x + _L0_gnn_ref(x, L0_gnn_W_in, L0_gnn_b_in, L0_gnn_W_agg, L0_gnn_W_self, L0_gnn_b_hid, L0_gnn_W_out, L0_gnn_b_out, edge_index), axis=-1)
    return x

_drawn_inputs = setup_inputs


def setup_inputs(seed=0):
    import zlib

    import numpy as np

    out = dict(_drawn_inputs(seed))
    spreads = {'L0_gnn_b_in': (0.0, 0.1), 'L0_gnn_b_hid': (0.0, 0.1), 'L0_gnn_b_out': (0.0, 0.1)}
    factors = {}
    for name, (base, spread) in spreads.items():
        noise = np.random.default_rng([zlib.crc32(name.encode()), seed]).standard_normal(out[name].shape)
        drawn = base * np.exp(spread * noise) if base else spread * noise
        out[name] = jnp.asarray(drawn.astype(out[name].dtype))
    for name, factor in factors.items():
        out[name] = (out[name] * factor).astype(out[name].dtype)
    return out
```

```python
import numpy as np
import concourse.bass as bass
from concourse import mybir
from contextlib import ExitStack

F32 = mybir.dt.float32
F32R = mybir.dt.float32r
BF16 = mybir.dt.bfloat16
F16 = mybir.dt.float16
I32 = mybir.dt.int32
ALU = mybir.AluOpType
ACT = mybir.ActivationFunctionType

P = 128
D = 256
C = D // P
TPG = 4
GROUP = P * TPG
LAYERS = 3
EPS = 1e-5
FAR = 1 << 20


WIDE = 2 * D


class Memory:
    pass


def wait(engine, sem, count):
    if isinstance(count, int) and count <= 0:
        return
    engine.wait_ge(sem, count)


def run_iterations(engine, n, body):
    body(0)
    if n > 2:
        with engine.Fori(1, n - 1) as i:
            body(i)
    body(n - 1)


def group_of(table, g):
    return table[bass.ds(g * GROUP, GROUP), :].rearrange("(p j) d -> p (j d)", j=TPG)


def last_group_of(m, table):
    return table[(m.NG - 1) * GROUP:m.N, :].rearrange("(p j) d -> p (j d)", j=TPG)


def prepare_constants_and_weights(nc, m):
    EK, EFULL, EREST = m.EK, m.EFULL, m.EREST
    with ExitStack() as ctx:
        def sem(name):
            return ctx.enter_context(nc.semaphore("prep_" + name))

        w_in_s, rows_s, edges_s = sem("weights_in"), sem("rows_in"), sem("edges_in")
        const_s, dve_s, act_s, pe_s = sem("constants"), sem("dve"), sem("act"), sem("pe")
        parts_s, bo3_s, pads_s = sem("b_out_parts"), sem("b_out_3"), sem("edge_pads")
        bin_s, win_t_s = sem("b_in_spread"), sem("w_in_transposed")
        block = ctx.enter_context(nc.Block())

        @block.sync
        def _(sp):
            sp.dma_start(m.win_f[:, :, :], m.w_in.rearrange("(c p) n -> p c n", p=P)).then_inc(w_in_s, 16)
            for l in range(LAYERS):
                sp.dma_start(m.w_f[l][:, :, 0:D],
                             m.w_self[l].rearrange("(c p) n -> p c n", p=P)).then_inc(w_in_s, 16)
                sp.dma_start(m.w_f[l][:, :, D:WIDE],
                             m.w_agg[l].rearrange("(c p) n -> p c n", p=P)).then_inc(w_in_s, 16)
            sp.dma_start(m.w_f[LAYERS][:, :, :],
                         m.w_out.rearrange("(c p) n -> p c n", p=P)).then_inc(w_in_s, 16)
            sp.dma_start(m.brows[0:1, :], m.b_hid.rearrange("(o l) n -> o (l n)", o=1)).then_inc(rows_s, 16)
            sp.dma_start(m.bo_row[0:1, :], m.b_out.rearrange("(o n) -> o n", o=1)).then_inc(rows_s, 16)
            with nc.allow_non_contiguous_dma(reason="256 numbers"):
                sp.dma_start(m.bin_c[:, :], m.b_in.rearrange("(c p) -> p c", p=P)).then_inc(rows_s, 16)
            sp.wait_ge(pads_s, 2)
            for column, array in ((m.tgt_i, m.src), (m.src_i, m.dst)):
                even = EFULL // 16 * 16
                for a, b in ((0, even), (even, EFULL)):
                    if b > a:
                        sp.dma_start(column[a:b, :],
                                     array[a * EK:b * EK].rearrange("(p k) -> p k", k=EK)).then_inc(edges_s, 16)
                if EREST:
                    sp.dma_start(column[EFULL:EFULL + 1, 0:EREST],
                                 array[EFULL * EK:EFULL * EK + EREST].rearrange("(o k) -> o k", o=1)
                                 ).then_inc(edges_s, 16)
            sp.wait_ge(parts_s, 1)
            sp.dma_start(m.bo_3[:, :], m.bo_parts[0:1, :, :]).then_inc(bo3_s, 16)
            sp.wait_ge(bo3_s, 16)

        edge_loads = 2 * ((EFULL >= 16) + (EFULL % 16 > 0) + (EREST > 0))

        @block.gpsimd
        def _(pool):
            g = nc.gpsimd
            g.memset(m.tgt_i[:, :], m.NROW).then_inc(pads_s, 1)
            g.memset(m.src_i[:, :], 0).then_inc(pads_s, 1)
            g.memset(m.ident[:, :], 0.0).then_inc(const_s, 1)
            g.memset(m.ones_f[:, :], 1.0).then_inc(const_s, 1)
            g.memset(m.zeros_b[:, :], 0.0).then_inc(const_s, 1)
            g.memset(m.ones_b[:, :], 1.0).then_inc(const_s, 1)
            g.memset(m.gath[:, :, :], 0.0).then_inc(const_s, 1)
            g.memset(m.in_buf[:, :, :], 0.0).then_inc(const_s, 1)
            g.memset(m.x_buf[:, :, :], 0.0).then_inc(const_s, 1)
            g.iota(m.iota_i[:, :], pattern=[[1, max(m.NT, P)]], base=0, channel_multiplier=0).then_inc(const_s, 1)
            pool.wait_ge(const_s, 8)
            g.affine_select(out=m.ident[:, :], in_=m.ident[:, :], compare_op=ALU.not_equal, fill=1.0, base=0,
                            pattern=[[-1, P]], channel_multiplier=1).then_inc(const_s, 1)
            g.affine_select(out=m.after_f[:, :], in_=m.ones_f[:, :], compare_op=ALU.is_gt, fill=0.0, base=0,
                            pattern=[[-1, P]], channel_multiplier=1).then_inc(const_s, 1)
            g.affine_select(out=m.before[:, :], in_=m.ones_f[:, :], compare_op=ALU.is_gt, fill=0.0, base=0,
                            pattern=[[1, P]], channel_multiplier=-1).then_inc(const_s, 1)

        @block.scalar
        def _(act):
            act.wait_ge(w_in_s, 16 * (2 + 2 * LAYERS))
            for l in range(1, LAYERS + 1):
                nc.scalar.activation(m.w_hi[l][:, :, :], m.w_f[l][:, :, :], ACT.Copy).then_inc(act_s, 1)
            act.wait_ge(pe_s, 2)
            nc.scalar.activation(m.w_hi[0][:, :, :], m.ps[:, 1:3, :], ACT.Copy).then_inc(act_s, 1)

        @block.vector
        def _(dve):
            v = nc.vector
            chain = [0]

            def link(ins):
                chain[0] += 1
                ins.then_inc(dve_s, 1)
                dve.wait_ge(dve_s, chain[0])

            dve.wait_ge(const_s, 11)
            v.tensor_copy(m.iota_f[:, :], m.iota_i[:, 0:P])
            v.tensor_copy(m.iota_h[:, :], m.iota_i[:, 0:m.NT])
            v.tensor_scalar(m.notbefore[:, :], m.before[:, :], -1.0, 1.0, ALU.mult, ALU.add)
            dve.wait_ge(rows_s, 48)
            for c in range(C):
                last = v.tensor_scalar(m.bin_b[:, c, :], m.ones_f[:, :], m.bin_c[:, c:c + 1], None, ALU.mult)
            last.then_inc(bin_s, 1)
            link(v.tensor_copy(m.bo_parts[0:1, 0, :], m.bo_row[0:1, :]))
            link(v.tensor_tensor(m.bo_rest[0:1, 0, :], m.bo_row[0:1, :], m.bo_parts[0:1, 0, :], ALU.subtract))
            link(v.tensor_copy(m.bo_parts[0:1, 1, :], m.bo_rest[0:1, 0, :]))
            link(v.tensor_tensor(m.bo_rest[0:1, 1, :], m.bo_rest[0:1, 0, :], m.bo_parts[0:1, 1, :],
                                 ALU.subtract))
            v.tensor_copy(m.bo_parts[0:1, 2, :], m.bo_rest[0:1, 1, :]).then_inc(parts_s, 1)
            dve.wait_ge(edges_s, 16 * edge_loads)
            v.tensor_copy(m.tgt_f[:, :], m.tgt_i[:, :])
            v.tensor_scalar(m.e_tmp[:, :], m.tgt_i[:, :], 9, 2, ALU.logical_shift_right, ALU.logical_shift_left)
            link(v.tensor_scalar(m.e_tmp2[:, :], m.tgt_i[:, :], 3, None, ALU.bitwise_and))
            link(v.tensor_tensor(m.bucket_f[:, :], m.e_tmp[:, :], m.e_tmp2[:, :], ALU.add))
            link(v.tensor_scalar(m.e_tmp[:, :], m.tgt_i[:, :], 2, P - 1, ALU.logical_shift_right, ALU.bitwise_and))
            link(v.tensor_copy(m.lo_f[:, :], m.e_tmp[:, :]))
            v.tensor_scalar(m.lo1_f[:, :], m.lo_f[:, :], 1.0, 65536.0, ALU.add, ALU.mult)
            link(v.tensor_scalar(m.e_tmp2[:, :], m.src_i[:, :], 255, None, ALU.bitwise_and))
            link(v.tensor_copy(m.src_lo_f[:, :], m.e_tmp2[:, :]))
            link(v.tensor_scalar(m.e_tmp[:, :], m.src_i[:, :], 8, None, ALU.logical_shift_right))
            link(v.tensor_scalar(m.src_hi_f[:, :], m.e_tmp[:, :], 256.0, None, ALU.mult))
            for l in range(1, LAYERS + 1):
                dve.wait_ge(act_s, l)
                v.tensor_tensor(m.w_lo[l][:, :, :], m.w_f[l][:, :, :], m.w_hi[l][:, :, :].bitcast(F32), ALU.subtract)
            dve.wait_ge(pe_s, 1)
            v.tensor_copy(m.winT[:, :, :].rearrange("p c n -> p (c n)"), m.ps[:, 0, :]).then_inc(win_t_s, 1)
            dve.wait_ge(act_s, LAYERS + 1)
            v.tensor_tensor(m.w_lo[0][:, :, :], m.ps[:, 1:3, :], m.w_hi[0][:, :, :].bitcast(F32), ALU.subtract)
            dve.wait_ge(pe_s, 3)
            link(v.tensor_copy(m.bias0[:, :], m.ps[:, 3, :]))
            v.tensor_tensor(m.bias0[:, 0:D], m.bias0[:, 0:D], m.ps[:, 4, 0:D], ALU.add)
            for l in (1, 2):
                for t in range(2):
                    v.tensor_copy(m.bias_p[l][:, t, :], m.ps[:, 4 + l // 2, (l % 2) * D:(l % 2) * D + D])

        @block.tensor
        def _(pe):
            t = nc.tensor
            pe.wait_ge(w_in_s, 16 * (2 + 2 * LAYERS))
            pe.wait_ge(const_s, 11)
            for h in range(C):
                for c in range(C):
                    last = t.transpose(m.ps[:, 0, h * D + c * P:h * D + (c + 1) * P],
                                       m.win_f[:, c, h * P:(h + 1) * P], m.ident[:, :])
            last.then_inc(pe_s, 1)
            pe.wait_ge(win_t_s, 1)
            for c in range(C):
                for h in range(C):
                    last = t.matmul(m.ps[:, 1 + c, :], m.winT[:, h, c * P:(c + 1) * P], m.w_f[0][:, h, :],
                                    start=h == 0, stop=h == C - 1)
            last.then_inc(pe_s, 1)
            pe.wait_ge(bin_s, 1)
            for h in range(C):
                t.matmul(m.ps[:, 3, :], m.bin_b[:, h, :], m.w_f[0][:, h, :], start=h == 0, stop=h == C - 1)
            pe.wait_ge(rows_s, 48)
            t.matmul(m.ps[:, 4, :], m.ones_f[0:1, :], m.brows[0:1, 0:2 * D], start=True, stop=True)
            t.matmul(m.ps[:, 5, 0:D], m.ones_f[0:1, :], m.brows[0:1, 2 * D:3 * D],
                     start=True, stop=True).then_inc(pe_s, 1)


def split_products(nc, m, out_ap, slot, tile, layer, start=True):
    n = 0
    for c in range(C):
        for h, w in ((m.hT_hi, m.w_hi), (m.hT_hi, m.w_lo), (m.hT_lo, m.w_hi)):
            last = nc.tensor.matmul(out_ap, h[:, slot, tile, c, :], w[layer][:, c, :],
                                    start=start and n == 0, stop=n == 3 * C - 1)
            n += 1
    return last


def first_pass_and_buckets(nc, m):
    NT, NI, EK = m.NT, m.NI, m.EK
    RANK, DEG, SLOT, HT, O = 0, 1, 2, 3, 5
    with ExitStack() as ctx:
        def sem(name):
            return ctx.enter_context(nc.semaphore("p0_" + name))

        x_in = [sem(f"x_in{q}") for q in range(2)]
        stored = [sem(f"stored{q}") for q in range(2)]
        transposed, hi_done, lo_done = sem("transposed"), sem("hi_done"), sem("lo_done")
        multiplied, evacuated = sem("multiplied"), sem("evacuated")
        onehot_done, ranked = sem("onehot_done"), sem("ranked")
        rank_read, at_slot_done, counted = sem("rank_read"), sem("at_slot_done"), sem("counted")
        block = ctx.enter_context(nc.Block())

        @block.sync
        def _(sp):
            def load(g, q):
                sp.dma_start(m.in_buf[:, q, :], group_of(m.x, g)).then_inc(x_in[q], 16)

            def body(i):
                for q in range(2):
                    g = 2 * i + q
                    wait(sp, evacuated, TPG * g + TPG)
                    sp.dma_start(group_of(m.p_tab[0], g), m.p_out[:, q, :]).then_inc(stored[q], 16)
                    sp.dma_start(m.t_tab[0][bass.ds(g * GROUP, GROUP), :].rearrange("(p j) d -> p (j d)", j=TPG),
                                 m.t_out[:, q, :]).then_inc(stored[q], 16)
                    if isinstance(i, int) and i == NI - 2 and q == 1:
                        sp.dma_start(m.in_buf[0:m.LASTP, q, :], last_group_of(m, m.x)).then_inc(x_in[q], 16)
                    elif not (isinstance(i, int) and i == NI - 1):
                        load(g + 2, q)

            load(0, 0)
            load(1, 1)
            body(0)
            if NI > 3:
                with sp.Fori(1, NI - 2) as i:
                    body(i)
            body(NI - 2)
            body(NI - 1)
            for q in range(2):
                sp.wait_ge(stored[q], 32 * NI)

        @block.scalar
        def _(act):
            def split_hi(t, r):
                wait(act, transposed, t + 1)
                wait(act, multiplied, t - 3)
                nc.scalar.activation(m.hT_hi[:, (r // 2) % 2, r % 2, :, :],
                                     m.ps[:, HT + r % 2, 0:D], ACT.Copy).then_inc(hi_done, 1)

            def body(i):
                for j in range(8):
                    if not (isinstance(i, int) and i == NI - 1 and j == 7):
                        split_hi(8 * i + j + 1, j + 1)

            split_hi(0, 0)
            run_iterations(act, NI, body)

        @block.vector
        def _(dve):
            v = nc.vector

            def split_lo(t, r):
                wait(dve, hi_done, t + 1)
                wait(dve, multiplied, t - 3)
                hi = m.hT_hi[:, (r // 2) % 2, r % 2, :, :].rearrange("p c n -> p (c n)").bitcast(F32)
                v.tensor_tensor(m.hT_lo[:, (r // 2) % 2, r % 2, :, :].rearrange("p c n -> p (c n)"),
                                m.ps[:, HT + r % 2, 0:D], hi, ALU.subtract).then_inc(lo_done, 1)

            def onehots(k, q):
                wait(dve, counted, k - 1)
                v.tensor_scalar(m.oh_bucket[:, q, :], m.iota_h[:, :], m.bucket_f[:, bass.ds(k, 1)], None,
                                ALU.is_equal)
                v.tensor_scalar(m.oh_lo[:, q, :], m.iota_f[:, :], m.lo_f[:, bass.ds(k, 1)], None,
                                ALU.is_equal).then_inc(onehot_done, 1)

            def slots(k, q):
                wait(dve, ranked, k + 1)
                v.tensor_tensor_reduce(out=m.junk[:, :], in0=m.ps[:, RANK, 0:NT], in1=m.oh_bucket[:, q, :],
                                       scale=1.0, scalar=0.0, op0=ALU.mult, op1=ALU.add,
                                       accum_out=m.rank[:, q:q + 1]).then_inc(rank_read, 1)
                wait(dve, rank_read, k + 1)
                for n, number in enumerate((m.lo1_f, m.src_lo_f, m.src_hi_f)):
                    last = v.tensor_scalar(m.at_slot[:, q, n, :], m.iota_f[:, :], m.rank[:, q:q + 1],
                                           number[:, bass.ds(k, 1)], ALU.is_equal, ALU.mult)
                last.then_inc(at_slot_done, 1)

            def evacuate(t, i, j):
                q = j // TPG
                wait(dve, multiplied, t + 1)
                if j % TPG == 0:
                    wait(dve, stored[q], 32 * i)
                c = (j % TPG) * D
                v.tensor_tensor(m.p_out[:, q, c:c + D], m.ps[:, O + j % 2, 0:D], m.bias0[:, 0:D], ALU.add)
                v.tensor_tensor(m.t_out[:, q, c:c + D], m.ps[:, O + j % 2, D:WIDE], m.bias0[:, D:WIDE],
                                ALU.add).then_inc(evacuated, 1)

            def body(i):
                final = isinstance(i, int) and i == NI - 1
                for j in range(8):
                    t = 8 * i + j
                    k = 4 * i + j // 2
                    if not (final and j == 7):
                        split_lo(t + 1, j + 1)
                    if j % 2 == 0:
                        slots(k, (j // 2) % 2)
                    elif not (final and j == 7):
                        onehots(k + 1, (j // 2 + 1) % 2)
                    evacuate(t, i, j)

            onehots(0, 0)
            split_lo(0, 0)
            run_iterations(dve, NI, body)

        @block.tensor
        def _(pe):
            def transposes(t, i, r):
                if r % TPG == 0:
                    wait(pe, x_in[(r // TPG) % 2], 16 * i + 16)
                wait(pe, hi_done, t - 1)
                wait(pe, lo_done, t - 1)
                src = m.in_buf[:, (r // TPG) % 2, (r % TPG) * D:(r % TPG) * D + D]
                for c in range(C):
                    last = nc.tensor.transpose(m.ps[:, HT + r % 2, c * P:(c + 1) * P],
                                               src[:, c * P:(c + 1) * P], m.ident[:, :])
                last.then_inc(transposed, 1)

            def counts(bank, lhs, q):
                return nc.tensor.matmul(m.ps[:, bank, 0:NT], lhs, m.oh_bucket[:, q, :], start=False, stop=True,
                                        skip_group_check=True)

            def body(i):
                final = isinstance(i, int) and i == NI - 1
                for j in range(8):
                    t = 8 * i + j
                    k = 4 * i + j // 2
                    q = (j // 2) % 2
                    if j % 2 == 0:
                        wait(pe, onehot_done, k + 1)
                        counts(RANK, m.before[:, :], q).then_inc(ranked, 1)
                    if not (final and j == 7):
                        transposes(t + 1, i + (j + 1) // 8, (j + 1) % 8)
                    if j % 2 == 1:
                        wait(pe, at_slot_done, k + 1)
                        counts(RANK, m.notbefore[:, :], q)
                        counts(DEG, m.oh_lo[:, q, :], q)
                        for n in range(3):
                            last = counts(SLOT, m.at_slot[:, q, n, :], q)
                        last.then_inc(counted, 1)
                    wait(pe, hi_done, t + 1)
                    wait(pe, lo_done, t + 1)
                    wait(pe, evacuated, t - 1)
                    split_products(nc, m, m.ps[:, O + j % 2, :], (j // 2) % 2, j % 2, 0).then_inc(multiplied, 1)

            for bank in (RANK, DEG, SLOT):
                nc.tensor.matmul(m.ps[:, bank, 0:NT], m.zeros_b[:, 0:P], m.zeros_b[:, 0:NT], start=True, stop=True,
                                 skip_group_check=True)
            transposes(0, 0, 0)
            run_iterations(pe, NI, body)


def finish_tables(nc, m):
    RANK, DEG, SLOT = 0, 1, 2
    NT = m.NT
    with ExitStack() as ctx:
        dve_s = ctx.enter_context(nc.semaphore("tab_dve"))
        block = ctx.enter_context(nc.Block())

        @block.vector
        def _(dve):
            v = nc.vector
            chain = [0]

            def link(ins):
                chain[0] += 1
                ins.then_inc(dve_s, 1)
                dve.wait_ge(dve_s, chain[0])

            link(v.tensor_scalar(m.tab_a[:, :], m.ps[:, DEG, 0:NT], 1.0, None, ALU.max))
            v.reciprocal(m.inv_deg[:, :], m.tab_a[:, :])
            link(v.tensor_scalar(m.full_m[:, :], m.ps[:, RANK, 0:NT], float(P), None, ALU.is_gt))
            link(v.reduce_max(m.flag_f[:, :], m.full_m[:, :], mybir.AxisListType.X))
            link(v.tensor_copy(m.flag_i[:, :], m.flag_f[:, :]))
            link(v.tensor_copy(m.slot_i[:, :], m.ps[:, SLOT, 0:NT]))
            link(v.tensor_scalar(m.slot_src[:, :], m.slot_i[:, :], 16, None, ALU.logical_shift_right))
            link(v.tensor_copy(m.slot_lo[:, :], m.slot_src[:, :]))
            link(v.tensor_scalar(m.slot_lo[:, :], m.slot_lo[:, :], -1.0, None, ALU.add))
            link(v.tensor_scalar(m.slot_i[:, :], m.slot_i[:, :], 65535, None, ALU.bitwise_and))
            link(v.tensor_copy(m.tab_a[:, :], m.slot_i[:, :]))
            link(v.tensor_scalar(m.tab_b[:, :], m.slot_lo[:, :], 0.0, float(FAR), ALU.is_lt, ALU.mult))
            link(v.tensor_tensor(m.tab_a[:, :], m.tab_a[:, :], m.tab_b[:, :], ALU.add))
            link(v.tensor_scalar(m.tab_b[:, :], m.full_m[:, :], float(FAR), None, ALU.mult))
            link(v.tensor_tensor(m.tab_a[:, :], m.tab_a[:, :], m.tab_b[:, :], ALU.add))
            link(v.tensor_copy(m.slot_src[:, :], m.tab_a[:, :]))
            link(v.tensor_scalar(m.tab_b[:, :], m.full_m[:, :], float(-P), None, ALU.mult))
            link(v.tensor_tensor(m.slot_lo[:, :], m.slot_lo[:, :], m.tab_b[:, :], ALU.add))


def add_overfull_buckets(nc, m, layer):
    EK, NT, NROW = m.EK, m.NT, m.NROW
    TARGETS, SUMS, LO_T, WEIGHTS = 0, 1, 2, 3
    NEW, OLD = 0, 1
    STEPS = 8
    with ExitStack() as ctx:
        def sem(name):
            return ctx.enter_context(nc.semaphore(f"over{layer}_{name}"))

        turn, issue = sem("turn"), sem("issue")
        spread_done, targets_done, same_done = sem("spread_done"), sem("targets_done"), sem("same_done")
        weights_done, index_done = sem("weights_done"), sem("index_done")
        rows_in, old_in, written = sem("rows_in"), sem("old_in"), sem("written")
        summed, added, dve_s = sem("summed"), sem("added"), sem("dve")
        block = ctx.enter_context(nc.Block())

        def if_overfull(engine):
            flag = engine.value_load(m.flag_i[0:1, 0:1], min_val=0, max_val=1)
            return engine.If(flag)

        @block.gpsimd
        def _(pool):
            def indexed(out, out_offset, in_, in_offset, sem_):
                nc.gpsimd.indirect_dma_start(out=out, out_offset=out_offset, in_=in_, in_offset=in_offset,
                                             bounds_check=NROW - 1, oob_is_err=False).then_inc(sem_, 16)

            with if_overfull(pool):
                pool.sem_inc(turn, 1)
                with pool.Fori(0, EK) as k:
                    pool.wait_ge(spread_done, k + 1)
                    pool.sem_inc(issue, 1)
                    indexed(m.gath[:, NEW, :], None, m.t_tab[layer][:, :],
                            bass.IndirectOffsetOnAxis(ap=m.over_src[:, :], axis=0), rows_in)
                    pool.wait_ge(index_done, k + 1)
                    pool.sem_inc(issue, 1)
                    indexed(m.gath[:, OLD, :], None, m.p_tab[layer][:, :],
                            bass.IndirectOffsetOnAxis(ap=m.over_row[:, :], axis=0), old_in)
                    pool.wait_ge(added, k + 1)
                    pool.sem_inc(issue, 1)
                    indexed(m.p_tab[layer][:, :], bass.IndirectOffsetOnAxis(ap=m.over_row[:, :], axis=0),
                            m.v_buf[:, 0, 0, :], None, written)
                    pool.wait_ge(written, 16 * k + 16)
                    pool.sem_inc(turn, 1)

        @block.vector
        def _(dve):
            v = nc.vector
            with if_overfull(dve):
                with dve.Fori(0, EK) as k:
                    n = [0]

                    def link(ins):
                        n[0] += 1
                        ins.then_inc(dve_s, 1)
                        dve.wait_ge(dve_s, STEPS * k + n[0])

                    column = bass.ds(k, 1)
                    dve.wait_ge(turn, k + 1)
                    v.tensor_copy(m.over_src[:, :], m.src_i[:, column])
                    v.tensor_scalar(m.over_bucket[:, :], m.iota_h[:, :], m.bucket_f[:, column], None, ALU.is_equal)
                    v.tensor_scalar(m.over_lo[:, :], m.iota_f[:, :], m.lo_f[:, column], None, ALU.is_equal)
                    v.tensor_scalar(m.over_spread[:, :], m.ones_f[:, :], m.tgt_f[:, column], None,
                                    ALU.mult).then_inc(spread_done, 1)
                    dve.wait_ge(targets_done, k + 1)
                    v.tensor_copy(m.over_loT[:, :], m.ps[:, LO_T, 0:P])
                    v.tensor_scalar(m.over_same[:, :], m.ps[:, TARGETS, 0:P], m.tgt_f[:, column], None,
                                    ALU.is_equal).then_inc(same_done, 1)
                    dve.wait_ge(same_done, k + 1)
                    link(v.tensor_tensor_reduce(out=m.over_earlier[:, :], in0=m.over_same[:, :],
                                                in1=m.after_f[:, :], scale=1.0, scalar=0.0, op0=ALU.mult,
                                                op1=ALU.add, accum_out=m.over_n[:, 0:1]))
                    link(v.tensor_tensor_reduce(out=m.junk[:, :], in0=m.over_bucket[:, :], in1=m.full_m[:, :],
                                                scale=1.0, scalar=0.0, op0=ALU.mult, op1=ALU.add,
                                                accum_out=m.over_n[:, 1:2]))
                    link(v.tensor_scalar(m.over_n[:, 2:3], m.over_n[:, 0:1], 0.0, float(FAR), ALU.is_gt, ALU.mult))
                    link(v.tensor_scalar(m.over_n[:, 3:4], m.over_n[:, 1:2], float(-FAR), float(FAR), ALU.mult,
                                         ALU.add))
                    link(v.tensor_tensor(m.over_n[:, 2:3], m.over_n[:, 2:3], m.over_n[:, 3:4], ALU.add))
                    link(v.tensor_tensor(m.over_n[:, 2:3], m.over_n[:, 2:3], m.tgt_f[:, column], ALU.add))
                    v.tensor_copy(m.over_row[:, :], m.over_n[:, 2:3]).then_inc(index_done, 1)
                    dve.wait_ge(weights_done, k + 1)
                    link(v.tensor_tensor_reduce(out=m.junk[:, :], in0=m.ps[:, WEIGHTS, 0:NT],
                                                in1=m.over_bucket[:, :], scale=1.0, scalar=0.0, op0=ALU.mult,
                                                op1=ALU.add, accum_out=m.over_n[:, 4:5]))
                    dve.wait_ge(summed, k + 1)
                    dve.wait_ge(old_in, 16 * k + 16)
                    link(v.tensor_scalar(m.v_buf[:, 0, 1, :], m.ps[:, SUMS, 0:D], m.over_n[:, 4:5], None, ALU.mult))
                    v.tensor_tensor(m.v_buf[:, 0, 0, :], m.v_buf[:, 0, 1, :], m.gath[:, OLD, :],
                                    ALU.add).then_inc(added, 1)
                    assert n[0] == STEPS

        @block.tensor
        def _(pe):
            with if_overfull(pe):
                with pe.Fori(0, EK) as k:
                    pe.wait_ge(spread_done, k + 1)
                    nc.tensor.matmul(m.ps[:, TARGETS, 0:P], m.over_spread[:, :], m.ident[:, :],
                                     start=True, stop=True)
                    nc.tensor.transpose(m.ps[:, LO_T, 0:P], m.over_lo[:, :], m.ident[:, :]).then_inc(targets_done, 1)
                    pe.wait_ge(same_done, k + 1)
                    nc.tensor.matmul(m.ps[:, WEIGHTS, 0:NT], m.over_loT[:, :], m.inv_deg[:, :],
                                     start=True, stop=True).then_inc(weights_done, 1)
                    pe.wait_ge(rows_in, 16 * k + 16)
                    nc.tensor.matmul(m.ps[:, SUMS, 0:D], m.over_same[:, :], m.gath[:, NEW, :],
                                     start=True, stop=True).then_inc(summed, 1)


class GatheringPass:

    def __init__(self, nc, m, layer, sem):
        self.nc, self.m, self.layer = nc, m, layer
        self.p_in = [sem(f"p_in{q}") for q in range(2)]
        self.gathered = [sem(f"gathered{r}") for r in range(8)]
        self.index_done = sem("index_done")
        self.issue = sem("issue")
        self.gath_hi_done, self.gath_lo_done = sem("gath_hi_done"), sem("gath_lo_done")
        self.picked, self.summed, self.v_done = sem("picked"), sem("summed"), sem("v_done")
        self.transposed, self.hi_done, self.lo_done = sem("transposed"), sem("hi_done"), sem("lo_done")
        self.multiplied = sem("multiplied")

    def at(self, i, j, ahead):
        u = 4 * i + j + ahead
        if isinstance(u, int) and not 0 <= u < 4 * self.m.NI:
            return None
        return u, i + (j + ahead) // 4, (j + ahead) % 4

    def run(self, engine, step, flush=0):
        NI = self.m.NI
        for j in range(1, 4):
            step(-1, j)

        def body(i):
            for j in range(4):
                step(i, j)

        run_iterations(engine, NI, body)
        for j in range(flush):
            step(NI, j)

    def gather_program(self, pool):
        m, nc = self.m, self.nc

        def body(i):
            for h in range(2):
                wait(pool, self.gath_lo_done, 4 * i + 2 * h - 2)
                pool.sem_inc(self.issue, 1)
                nc.gpsimd.tensor_copy(m.idx8[:, h, 0:4],
                                      m.slot_src[:, bass.ds(8 * i + 4 * h, 4)]).then_inc(self.index_done, 1)
                wait(pool, self.index_done, 2 * i + h + 1)
                pool.sem_inc(self.issue, 1)
                for n in range(4):
                    nc.gpsimd.indirect_dma_start(
                        out=m.gath[:, 4 * h + n, :], out_offset=None, in_=m.t_tab[self.layer - 1][:, :],
                        in_offset=bass.IndirectOffsetOnAxis(ap=m.idx8[:, h, n:n + 1], axis=0),
                        bounds_check=m.NROW - 1, oob_is_err=False).then_inc(self.gathered[4 * h + n], 16)

        run_iterations(pool, m.NI, body)

    def split_hi(self, act, i, j):
        m = self.m
        if place := self.at(i, j, 1):
            u, _, r = place
            wait(act, self.transposed, u + 1)
            wait(act, self.multiplied, u - 1)
            self.nc.scalar.activation(m.hT_hi[:, r % 2, :, :, :].rearrange("p t c n -> p (t c n)"),
                                      m.ps[:, 2 + r % 2, :], ACT.Relu).then_inc(self.hi_done, 1)

    def split_gathered_hi(self, act, i, j):
        m = self.m
        if place := self.at(i, j, 3):
            u, n, r = place
            for q in (2 * r, 2 * r + 1):
                wait(act, self.gathered[q], 16 * n + 16)
            wait(act, self.summed, u - 1)
            wait(act, self.gath_lo_done, u - 1)
            self.nc.scalar.activation(m.gath_hi[:, r % 2, :, :], m.gath[:, 2 * r:2 * r + 2, :],
                                      ACT.Copy).then_inc(self.gath_hi_done, 1)

    def split_lo(self, dve, i, j):
        m = self.m
        if place := self.at(i, j, 1):
            u, _, r = place
            wait(dve, self.hi_done, u + 1)
            self.nc.vector.scalar_tensor_tensor(
                out=m.hT_lo[:, r % 2, :, :, :].rearrange("p t c n -> p (t c n)"), in0=m.ps[:, 2 + r % 2, :],
                scalar=0.0, in1=m.hT_hi[:, r % 2, :, :, :].rearrange("p t c n -> p (t c n)").bitcast(F32),
                op0=ALU.max, op1=ALU.subtract).then_inc(self.lo_done, 1)

    def make_v(self, dve, i, j):
        m = self.m
        if place := self.at(i, j, 2):
            u, n, r = place
            if r % 2 == 0:
                wait(dve, self.p_in[r // 2], 16 * n + 16)
            wait(dve, self.summed, u + 1)
            wait(dve, self.transposed, u - 1)
            for t in range(2):
                c = (2 * (r % 2) + t) * D
                last = self.nc.vector.scalar_tensor_tensor(
                    out=m.v_buf[:, r % 2, t, :], in0=m.ps[:, r % 2, t * D:(t + 1) * D],
                    scalar=m.inv_deg[:, bass.ds(2 * u + t, 1)], in1=m.in_buf[:, r // 2, c:c + D],
                    op0=ALU.mult, op1=ALU.add)
            last.then_inc(self.v_done, 1)

    def split_gathered_lo(self, dve, i, j):
        m = self.m
        if place := self.at(i, j, 3):
            u, _, r = place
            wait(dve, self.gath_hi_done, u + 1)
            self.nc.vector.tensor_tensor(m.gath_lo[:, r % 2, :, :], m.gath[:, 2 * r:2 * r + 2, :],
                                         m.gath_hi[:, r % 2, :, :].bitcast(F32),
                                         ALU.subtract).then_inc(self.gath_lo_done, 1)

    def make_pick(self, dve, i, j):
        m = self.m
        if place := self.at(i, j, 3):
            u, _, r = place
            wait(dve, self.summed, u - 1)
            for t in range(2):
                last = self.nc.vector.tensor_scalar(m.pick[:, r % 2, t, :], m.iota_f[:, :],
                                                    m.slot_lo[:, bass.ds(2 * u + t, 1)], None, ALU.is_equal)
            last.then_inc(self.picked, 1)

    def sum_per_node(self, pe, i, j):
        m = self.m
        if place := self.at(i, j, 2):
            u, _, r = place
            wait(pe, self.gath_lo_done, u + 1)
            wait(pe, self.picked, u + 1)
            wait(pe, self.v_done, u - 1)
            for t in range(2):
                for n, rows in enumerate((m.gath_hi, m.gath_lo)):
                    last = self.nc.tensor.matmul(m.ps[:, r % 2, t * D:(t + 1) * D], m.pick[:, r % 2, t, :],
                                                 rows[:, r % 2, t, :], start=n == 0, stop=n == 1)
            last.then_inc(self.summed, 1)

    def transpose_v(self, pe, i, j):
        m = self.m
        if place := self.at(i, j, 1):
            u, _, r = place
            wait(pe, self.v_done, u + 1)
            wait(pe, self.lo_done, u - 1)
            for t in range(2):
                for c in range(C):
                    last = self.nc.tensor.transpose(m.ps[:, 2 + r % 2, (2 * t + c) * P:(2 * t + c + 1) * P],
                                                    m.v_buf[:, r % 2, t, c * P:(c + 1) * P], m.ident[:, :])
            last.then_inc(self.transposed, 1)


def middle_pass(nc, m, layer):
    NI = m.NI
    with ExitStack() as ctx:
        def sem(name):
            return ctx.enter_context(nc.semaphore(f"p{layer}_{name}"))

        g = GatheringPass(nc, m, layer, sem)
        stored = [sem(f"stored{q}") for q in range(2)]
        p_evacuated, t_evacuated = sem("p_evacuated"), sem("t_evacuated")
        block = ctx.enter_context(nc.Block())

        @block.sync
        def _(sp):
            def load(group, q):
                sp.dma_start(m.in_buf[:, q, :], group_of(m.p_tab[layer - 1], group)).then_inc(g.p_in[q], 16)

            def body(i):
                for q in range(2):
                    group = 2 * i + q
                    if not (isinstance(i, int) and i == NI - 1):
                        wait(sp, g.v_done, 2 * group + 2)
                        load(group + 2, q)
                    wait(sp, p_evacuated, 2 * group + 2)
                    sp.dma_start(group_of(m.p_tab[layer], group), m.p_out[:, q, :]).then_inc(stored[q], 16)
                    wait(sp, t_evacuated, 2 * group + 2)
                    sp.dma_start(m.t_tab[layer][bass.ds(group * GROUP, GROUP), :]
                                 .rearrange("(p j) d -> p (j d)", j=TPG), m.t_out[:, q, :]).then_inc(stored[q], 16)

            load(0, 0)
            load(1, 1)
            run_iterations(sp, NI, body)
            for q in range(2):
                sp.wait_ge(stored[q], 32 * NI)

        @block.gpsimd
        def _(pool):
            g.gather_program(pool)

        @block.scalar
        def _(act):
            def evacuate_t(i, j):
                if place := g.at(i, j, 0):
                    u, n, r = place
                    wait(act, g.multiplied, u + 1)
                    if r % 2 == 0:
                        wait(act, stored[r // 2], 32 * n)
                    nc.scalar.activation(
                        m.t_out[:, r // 2, (r % 2) * WIDE:(r % 2 + 1) * WIDE].rearrange("p (t d) -> p t d", t=2),
                        m.ps[:, 4 + 2 * (r % 2):6 + 2 * (r % 2), D:WIDE], ACT.Copy).then_inc(t_evacuated, 1)

            def step(i, j):
                g.split_hi(act, i, j)
                g.split_gathered_hi(act, i, j)
                evacuate_t(i, j)

            g.run(act, step)

        @block.vector
        def _(dve):
            def evacuate_p(i, j):
                if place := g.at(i, j, 0):
                    u, n, r = place
                    wait(dve, t_evacuated, u + 1)
                    if r % 2 == 0:
                        wait(dve, stored[r // 2], 32 * n)
                    nc.vector.tensor_tensor(
                        m.p_out[:, r // 2, (r % 2) * WIDE:(r % 2 + 1) * WIDE].rearrange("p (t d) -> p t d", t=2),
                        m.ps[:, 4 + 2 * (r % 2):6 + 2 * (r % 2), 0:D], m.bias_p[layer][:, :, :],
                        ALU.add).then_inc(p_evacuated, 1)

            def step(i, j):
                g.split_lo(dve, i, j)
                g.make_v(dve, i, j)
                g.split_gathered_lo(dve, i, j)
                g.make_pick(dve, i, j)
                evacuate_p(i, j)

            g.run(dve, step)

        @block.tensor
        def _(pe):
            def multiply(i, j):
                if place := g.at(i, j, 0):
                    u, _, r = place
                    wait(pe, g.lo_done, u + 1)
                    wait(pe, p_evacuated, u - 1)
                    for t in range(2):
                        last = split_products(nc, m, m.ps[:, 4 + 2 * (r % 2) + t, :], r % 2, t, layer)
                    last.then_inc(g.multiplied, 1)

            def step(i, j):
                g.sum_per_node(pe, i, j)
                g.transpose_v(pe, i, j)
                multiply(i, j)

            g.run(pe, step)


def last_pass(nc, m):
    NI = m.NI
    with ExitStack() as ctx:
        def sem(name):
            return ctx.enter_context(nc.semaphore(f"p{LAYERS}_{name}"))

        g = GatheringPass(nc, m, LAYERS, sem)
        x_in = [sem(f"x_in{q}") for q in range(2)]
        stored = [sem(f"stored{q}") for q in range(2)]
        y_done, var_done, root_done = sem("y_done"), sem("var_done"), sem("root_done")
        scale_ready, scale_done, normed, dve_s = sem("scale_ready"), sem("scale_done"), sem("normed"), sem("dve")
        issue = sem("issue_aggregate")
        block = ctx.enter_context(nc.Block())

        @block.sync
        def _(sp):
            def load_p(group, q):
                sp.dma_start(m.in_buf[:, q, :], group_of(m.p_tab[LAYERS - 1], group)).then_inc(g.p_in[q], 16)

            def load_x(group, q, last):
                if last:
                    sp.dma_start(m.x_buf[0:m.LASTP, q, :], last_group_of(m, m.x)).then_inc(x_in[q], 16)
                else:
                    sp.dma_start(m.x_buf[:, q, :], group_of(m.x, group)).then_inc(x_in[q], 16)

            def body(i):
                for q in range(2):
                    group = 2 * i + q
                    if not (isinstance(i, int) and i == NI - 1):
                        wait(sp, g.v_done, 2 * group + 2)
                        load_p(group + 2, q)
                        wait(sp, y_done, 2 * group + 2)
                        load_x(group + 2, q, isinstance(i, int) and i == NI - 2 and q == 1)
                    wait(sp, normed, 2 * group + 2)
                    if isinstance(i, int) and i == NI - 1 and q == 1:
                        sp.dma_start(last_group_of(m, m.out), m.p_out[0:m.LASTP, q, :]).then_inc(stored[q], 16)
                    else:
                        sp.dma_start(group_of(m.out, group), m.p_out[:, q, :]).then_inc(stored[q], 16)

            for q in range(2):
                load_p(q, q)
                load_x(q, q, False)
            body(0)
            if NI > 3:
                with sp.Fori(1, NI - 2) as i:
                    body(i)
            body(NI - 2)
            body(NI - 1)
            for q in range(2):
                sp.wait_ge(stored[q], 16 * NI)

        @block.gpsimd
        def _(pool):
            g.gather_program(pool)

        @block.scalar
        def _(act):
            def root(i, j):
                if place := g.at(i, j, -1):
                    u, _, r = place
                    s = 2 * (r % 2)
                    wait(act, var_done, u + 1)
                    nc.scalar.activation(m.root[:, s:s + 2], m.ve[:, s:s + 2], ACT.Sqrt).then_inc(root_done, 1)

            def normalise(i, j):
                if place := g.at(i, j, -1):
                    u, n, r = place
                    wait(act, scale_done, u + 1)
                    if r % 2 == 0:
                        wait(act, stored[r // 2], 16 * n)
                    for t in range(2):
                        s = 2 * (r % 2) + t
                        last = nc.scalar.activation(m.p_out[:, r // 2, s * D:(s + 1) * D], m.y_buf[:, s, :],
                                                    ACT.Identity, bias=m.nmr[:, s:s + 1],
                                                    scale=m.rstd[:, s:s + 1])
                    last.then_inc(normed, 1)

            def step(i, j):
                g.split_hi(act, i, j)
                root(i, j)
                g.split_gathered_hi(act, i, j)
                normalise(i, j)

            g.run(act, step, flush=1)

        @block.vector
        def _(dve):
            v = nc.vector

            def residual(i, j):
                if place := g.at(i, j, 0):
                    u, n, r = place
                    s = 2 * (r % 2)
                    wait(dve, g.multiplied, u + 1)
                    if r % 2 == 0:
                        wait(dve, x_in[r // 2], 16 * n + 16)
                    wait(dve, normed, u - 1)
                    v.tensor_tensor(m.y_buf[:, s:s + 2, :],
                                    m.ps[:, 4 + r % 2, :].rearrange("p (t d) -> p t d", t=2),
                                    m.x_buf[:, r // 2, (r % 2) * WIDE:(r % 2 + 1) * WIDE]
                                    .rearrange("p (t d) -> p t d", t=2), ALU.add).then_inc(y_done, 1)
                    wait(dve, y_done, u + 1)
                    for t in range(2):
                        last = v.bn_stats(m.stats[:, s + t, :], m.y_buf[:, s + t, :])
                    last.then_inc(dve_s, 1)
                    wait(dve, dve_s, 6 * u + 1)
                    dve.sem_inc(issue, 1)
                    for t in range(2):
                        last = v.bn_aggr(m.mv[:, s + t, :], m.stats[:, s + t, :])
                    last.then_inc(dve_s, 1)
                    wait(dve, dve_s, 6 * u + 2)
                    v.tensor_scalar(m.ve[:, s:s + 2], m.mv[:, s:s + 2, 1], EPS, None, ALU.add).then_inc(var_done, 1)

            def scales(i, j):
                if place := g.at(i, j, -1):
                    u, _, r = place
                    s = slice(2 * (r % 2), 2 * (r % 2) + 2)
                    n = 6 * u + 2
                    wait(dve, root_done, u + 1)
                    v.reciprocal(m.rstd[:, s], m.root[:, s]).then_inc(dve_s, 1)
                    wait(dve, dve_s, n + 1)
                    v.tensor_tensor(m.newton[:, s], m.rstd[:, s], m.ve[:, s], ALU.mult).then_inc(dve_s, 1)
                    wait(dve, dve_s, n + 2)
                    v.tensor_tensor(m.newton[:, s], m.newton[:, s], m.rstd[:, s], ALU.mult).then_inc(dve_s, 1)
                    wait(dve, dve_s, n + 3)
                    v.tensor_scalar(m.newton[:, s], m.newton[:, s], -0.5, 1.5, ALU.mult, ALU.add).then_inc(dve_s, 1)
                    wait(dve, dve_s, n + 4)
                    v.tensor_tensor(m.rstd[:, s], m.rstd[:, s], m.newton[:, s], ALU.mult).then_inc(scale_ready, 1)
                    wait(dve, scale_ready, u + 1)
                    v.scalar_tensor_tensor(out=m.nmr[:, s], in0=m.mv[:, s, 0], scalar=-1.0, in1=m.rstd[:, s],
                                           op0=ALU.mult, op1=ALU.mult).then_inc(scale_done, 1)

            def step(i, j):
                g.split_lo(dve, i, j)
                g.make_v(dve, i, j)
                g.split_gathered_lo(dve, i, j)
                g.make_pick(dve, i, j)
                scales(i, j)
                residual(i, j)

            g.run(dve, step, flush=1)

        @block.tensor
        def _(pe):
            def multiply(i, j):
                if place := g.at(i, j, 0):
                    u, _, r = place
                    wait(pe, g.lo_done, u + 1)
                    wait(pe, y_done, u - 1)
                    for t in range(2):
                        o = m.ps[:, 4 + r % 2, t * D:(t + 1) * D]
                        nc.tensor.matmul(o, m.ones_b[0:3, :], m.bo_3[0:3, :], start=True, stop=False)
                        last = split_products(nc, m, o, r % 2, t, LAYERS, start=False)
                    last.then_inc(g.multiplied, 1)

            def step(i, j):
                g.sum_per_node(pe, i, j)
                g.transpose_v(pe, i, j)
                multiply(i, j)

            g.run(pe, step)


def build_program(nc, x, src, dst, w_in, b_in, w_agg, w_self, b_hid, w_out, b_out, out):
    m = Memory()
    N = x.shape[0]
    E = src.shape[0]
    NG = -(-N // GROUP)
    NT = NG * TPG
    NROW = NG * GROUP
    LASTP = (N - (NG - 1) * GROUP) // TPG
    EK = 2 * NG
    EFULL = E // EK
    EREST = E - EFULL * EK
    NI = NG // 2
    assert NG % 2 == 0 and NG >= 6 and E <= EK * P and NT <= 512 and NROW <= 65536
    assert N % TPG == 0 and NROW < FAR

    with ExitStack() as ctx:
        def sb(name, shape, dt):
            return ctx.enter_context(nc.sbuf_tensor(name, shape, dt))

        m.p_tab = [nc.dram_tensor(f"p_tab{l}", [NROW, D], F32, kind="Internal").ap() for l in range(LAYERS)]
        m.t_tab = [nc.dram_tensor(f"t_tab{l}", [NROW, D], F32, kind="Internal").ap() for l in range(LAYERS)]

        m.ident = sb("ident", [P, P], F32)
        m.iota_i = sb("iota_i", [P, max(NT, P)], I32)
        m.iota_f = sb("iota_f", [P, P], F32)
        m.iota_h = sb("iota_h", [P, NT], F16)
        m.before = sb("before", [P, P], BF16)
        m.notbefore = sb("notbefore", [P, P], BF16)
        m.after_f = sb("after_f", [P, P], F32)
        m.zeros_b = sb("zeros_b", [P, 512], BF16)
        m.ones_f = sb("ones_f", [P, P], F32)
        m.ones_b = sb("ones_b", [3, P], BF16)

        m.w_f = [sb(f"w_f{l}", [P, C, WIDE], F32) for l in range(LAYERS)]
        m.w_f.append(sb("wo_f", [P, C, D], F32))
        m.win_f = sb("win_f", [P, C, D], F32)
        m.winT = sb("winT", [P, C, D], F32)
        widths = [WIDE] * LAYERS + [D]
        m.w_hi = [sb(f"w_hi{l}", [P, C, widths[l]], F32R) for l in range(LAYERS + 1)]
        m.w_lo = [sb(f"w_lo{l}", [P, C, widths[l]], F32R) for l in range(LAYERS + 1)]
        m.brows = sb("brows", [1, 2 * D + D], F32)
        m.bo_row = sb("bo_row", [1, D], F32)
        m.bo_rest = sb("bo_rest", [1, 2, D], F32)
        m.bo_parts = sb("bo_parts", [1, 3, D], BF16)
        m.bo_3 = sb("bo_3", [3, D], BF16)
        m.bin_c = sb("bin_c", [P, C], F32)
        m.bin_b = sb("bin_b", [P, C, P], F32)
        m.bias0 = sb("bias0", [P, WIDE], F32)
        m.bias_p = [None] + [sb(f"bias_p{l}", [P, 2, D], F32) for l in (1, 2)]

        m.tgt_i = sb("tgt_i", [P, EK], I32)
        m.src_i = sb("src_i", [P, EK], I32)
        m.e_tmp = sb("e_tmp", [P, EK], I32)
        m.e_tmp2 = sb("e_tmp2", [P, EK], I32)
        m.tgt_f = sb("tgt_f", [P, EK], F32)
        m.bucket_f = sb("bucket_f", [P, EK], F32)
        m.lo_f = sb("lo_f", [P, EK], F32)
        m.lo1_f = sb("lo1_f", [P, EK], F32)
        m.src_lo_f = sb("src_lo_f", [P, EK], F32)
        m.src_hi_f = sb("src_hi_f", [P, EK], F32)
        m.slot_i = sb("slot_i", [P, NT], I32)
        m.slot_lo = sb("slot_lo", [P, NT], F32)
        m.slot_src = sb("slot_src", [P, NT], I32)
        m.inv_deg = sb("inv_deg", [P, NT], F32)
        m.full_m = sb("full_m", [P, NT], F32)
        m.tab_a = sb("tab_a", [P, NT], F32)
        m.tab_b = sb("tab_b", [P, NT], F32)
        m.flag_f = sb("flag_f", [P, 1], F32)
        m.flag_i = sb("flag_i", [P, 1], I32)

        m.in_buf = sb("in_buf", [P, 2, TPG * D], F32)
        m.x_buf = sb("x_buf", [P, 2, TPG * D], F32)
        m.p_out = sb("p_out", [P, 2, TPG * D], F32)
        m.t_out = sb("t_out", [P, 2, TPG * D], F32)
        m.hT_hi = sb("hT_hi", [P, 2, 2, C, P], F32R)
        m.hT_lo = sb("hT_lo", [P, 2, 2, C, P], F32R)
        m.gath = sb("gath", [P, 8, D], F32)
        m.gath_hi = sb("gath_hi", [P, 2, 2, D], F32R)
        m.gath_lo = sb("gath_lo", [P, 2, 2, D], F32R)
        m.idx8 = sb("idx8", [P, 2, 8], I32)
        m.pick = sb("pick", [P, 2, 2, P], F32R)
        m.v_buf = sb("v_buf", [P, 2, 2, D], F32)
        m.y_buf = sb("y_buf", [P, 4, D], F32)
        m.stats = sb("stats", [P, 4, 6], F32)
        m.mv = sb("mv", [P, 4, 2], F32)
        m.ve = sb("ve", [P, 4], F32)
        m.rstd = sb("rstd", [P, 4], F32)
        m.nmr = sb("nmr", [P, 4], F32)
        m.root = sb("root", [P, 4], F32)
        m.newton = sb("newton", [P, 4], F32)
        m.over_src = sb("over_src", [P, 1], I32)
        m.over_row = sb("over_row", [P, 1], I32)
        m.over_spread = sb("over_spread", [P, P], F32)
        m.over_bucket = sb("over_bucket", [P, NT], F32)
        m.over_lo = sb("over_lo", [P, P], F32)
        m.over_loT = sb("over_loT", [P, P], F32)
        m.over_earlier = sb("over_earlier", [P, P], F32)
        m.over_n = sb("over_n", [P, 5], F32)
        m.over_same = sb("over_same", [P, P], F32)
        m.oh_bucket = sb("oh_bucket", [P, 2, NT], BF16)
        m.oh_lo = sb("oh_lo", [P, 2, P], BF16)
        m.at_slot = sb("at_slot", [P, 2, 3, P], BF16)
        m.rank = sb("rank", [P, 2], F32)
        m.junk = sb("junk", [P, NT], F32)

        m.ps = ctx.enter_context(nc.psum_tensor("ps", [P, 8, 512], F32))

        m.N, m.NG, m.NT, m.NROW, m.LASTP = N, NG, NT, NROW, LASTP
        m.EK, m.EFULL, m.EREST, m.NI = EK, EFULL, EREST, NI
        m.x, m.src, m.dst, m.w_in, m.b_in, m.w_agg, m.w_self = x, src, dst, w_in, b_in, w_agg, w_self
        m.b_hid, m.w_out, m.b_out, m.out = b_hid, w_out, b_out, out

        prepare_constants_and_weights(nc, m)
        first_pass_and_buckets(nc, m)
        finish_tables(nc, m)
        for layer in (1, 2):
            add_overfull_buckets(nc, m, layer - 1)
            middle_pass(nc, m, layer)
        add_overfull_buckets(nc, m, LAYERS - 1)
        last_pass(nc, m)


_INS = ["x", "src", "dst", "L0_gnn_W_in", "L0_gnn_b_in", "L0_gnn_W_agg", "L0_gnn_W_self", "L0_gnn_b_hid",
        "L0_gnn_W_out", "L0_gnn_b_out"]


def kernel(**inputs):
    import concourse.bacc as bacc
    from concourse.bass_utils import run_bass_kernel_spmd

    nc = bacc.Bacc("TRN2", target_bir_lowering=False, num_devices=1)
    arrays, args = {}, []
    for name in _INS:
        a = np.ascontiguousarray(inputs[name])
        arrays[f"in_{name}"] = a
        args.append(nc.dram_tensor(f"in_{name}", a.shape, mybir.dt.from_np(a.dtype), kind="ExternalInput").ap())
    out = nc.dram_tensor("out_0", inputs["x"].shape, F32, kind="ExternalOutput").ap()
    build_program(nc, *args, out)
    result = run_bass_kernel_spmd(nc, [arrays], core_ids=[0])
    return result.results[0]["out_0"]
```

```python
import numpy as np
import concourse.bass as bass
from concourse import mybir
from contextlib import ExitStack

F32 = mybir.dt.float32
F32R = mybir.dt.float32r
BF16 = mybir.dt.bfloat16
F16 = mybir.dt.float16
I32 = mybir.dt.int32
ALU = mybir.AluOpType
ACT = mybir.ActivationFunctionType

P = 128
D = 256
C = D // P
TPG = 4
GROUP = P * TPG
LAYERS = 3
EPS = 1e-5
FAR = 1 << 20


WIDE = 2 * D


class Memory:
    pass


def wait(engine, sem, count):
    if isinstance(count, int) and count <= 0:
        return
    engine.wait_ge(sem, count)


def run_iterations(engine, n, body):
    body(0)
    if n > 2:
        with engine.Fori(1, n - 1) as i:
            body(i)
    body(n - 1)


def group_of(table, g):
    return table[bass.ds(g * GROUP, GROUP), :].rearrange("(p j) d -> p (j d)", j=TPG)


def last_group_of(m, table):
    return table[(m.NG - 1) * GROUP:m.N, :].rearrange("(p j) d -> p (j d)", j=TPG)


def prepare_constants_and_weights(nc, m):
    EK, EFULL, EREST = m.EK, m.EFULL, m.EREST
    with ExitStack() as ctx:
        def sem(name):
            return ctx.enter_context(nc.semaphore("prep_" + name))

        w_in_s, rows_s, edges_s = sem("weights_in"), sem("rows_in"), sem("edges_in")
        const_s, dve_s, act_s, pe_s = sem("constants"), sem("dve"), sem("act"), sem("pe")
        parts_s, bo3_s, pads_s = sem("b_out_parts"), sem("b_out_3"), sem("edge_pads")
        bin_s, win_t_s = sem("b_in_spread"), sem("w_in_transposed")
        block = ctx.enter_context(nc.Block())

        @block.sync
        def _(sp):
            sp.dma_start(m.win_f[:, :, :], m.w_in.rearrange("(c p) n -> p c n", p=P)).then_inc(w_in_s, 16)
            for l in range(LAYERS):
                sp.dma_start(m.w_f[l][:, :, 0:D],
                             m.w_self[l].rearrange("(c p) n -> p c n", p=P)).then_inc(w_in_s, 16)
                sp.dma_start(m.w_f[l][:, :, D:WIDE],
                             m.w_agg[l].rearrange("(c p) n -> p c n", p=P)).then_inc(w_in_s, 16)
            sp.dma_start(m.w_f[LAYERS][:, :, :],
                         m.w_out.rearrange("(c p) n -> p c n", p=P)).then_inc(w_in_s, 16)
            sp.dma_start(m.brows[0:1, :], m.b_hid.rearrange("(o l) n -> o (l n)", o=1)).then_inc(rows_s, 16)
            sp.dma_start(m.bo_row[0:1, :], m.b_out.rearrange("(o n) -> o n", o=1)).then_inc(rows_s, 16)
            with nc.allow_non_contiguous_dma(reason="256 numbers"):
                sp.dma_start(m.bin_c[:, :], m.b_in.rearrange("(c p) -> p c", p=P)).then_inc(rows_s, 16)
            sp.wait_ge(pads_s, 2)
            for column, array in ((m.tgt_i, m.src), (m.src_i, m.dst)):
                even = EFULL // 16 * 16
                for a, b in ((0, even), (even, EFULL)):
                    if b > a:
                        sp.dma_start(column[a:b, :],
                                     array[a * EK:b * EK].rearrange("(p k) -> p k", k=EK)).then_inc(edges_s, 16)
                if EREST:
                    sp.dma_start(column[EFULL:EFULL + 1, 0:EREST],
                                 array[EFULL * EK:EFULL * EK + EREST].rearrange("(o k) -> o k", o=1)
                                 ).then_inc(edges_s, 16)
            sp.wait_ge(parts_s, 1)
            sp.dma_start(m.bo_3[:, :], m.bo_parts[0:1, :, :]).then_inc(bo3_s, 16)
            sp.wait_ge(bo3_s, 16)

        edge_loads = 2 * ((EFULL >= 16) + (EFULL % 16 > 0) + (EREST > 0))

        @block.gpsimd
        def _(pool):
            g = nc.gpsimd
            g.memset(m.tgt_i[:, :], m.NROW).then_inc(pads_s, 1)
            g.memset(m.src_i[:, :], 0).then_inc(pads_s, 1)
            g.memset(m.ident[:, :], 0.0).then_inc(const_s, 1)
            g.memset(m.ones_f[:, :], 1.0).then_inc(const_s, 1)
            g.memset(m.zeros_b[:, :], 0.0).then_inc(const_s, 1)
            g.memset(m.ones_b[:, :], 1.0).then_inc(const_s, 1)
            g.memset(m.gath[:, :, :], 0.0).then_inc(const_s, 1)
            g.memset(m.in_buf[:, :, :], 0.0).then_inc(const_s, 1)
            g.memset(m.x_buf[:, :, :], 0.0).then_inc(const_s, 1)
            g.iota(m.iota_i[:, :], pattern=[[1, max(m.NT, P)]], base=0, channel_multiplier=0).then_inc(const_s, 1)
            pool.wait_ge(const_s, 8)
            g.affine_select(out=m.ident[:, :], in_=m.ident[:, :], compare_op=ALU.not_equal, fill=1.0, base=0,
                            pattern=[[-1, P]], channel_multiplier=1).then_inc(const_s, 1)
            g.affine_select(out=m.after_f[:, :], in_=m.ones_f[:, :], compare_op=ALU.is_gt, fill=0.0, base=0,
                            pattern=[[-1, P]], channel_multiplier=1).then_inc(const_s, 1)
            g.affine_select(out=m.before[:, :], in_=m.ones_f[:, :], compare_op=ALU.is_gt, fill=0.0, base=0,
                            pattern=[[1, P]], channel_multiplier=-1).then_inc(const_s, 1)

        @block.scalar
        def _(act):
            act.wait_ge(w_in_s, 16 * (2 + 2 * LAYERS))
            for l in range(1, LAYERS + 1):
                nc.scalar.activation(m.w_hi[l][:, :, :], m.w_f[l][:, :, :], ACT.Copy).then_inc(act_s, 1)
            act.wait_ge(pe_s, 2)
            nc.scalar.activation(m.w_hi[0][:, :, :], m.ps[:, 1:3, :], ACT.Copy).then_inc(act_s, 1)

        @block.vector
        def _(dve):
            v = nc.vector
            chain = [0]

            def link(ins):
                chain[0] += 1
                ins.then_inc(dve_s, 1)
                dve.wait_ge(dve_s, chain[0])

            dve.wait_ge(const_s, 11)
            v.tensor_copy(m.iota_f[:, :], m.iota_i[:, 0:P])
            v.tensor_copy(m.iota_h[:, :], m.iota_i[:, 0:m.NT])
            v.tensor_scalar(m.notbefore[:, :], m.before[:, :], -1.0, 1.0, ALU.mult, ALU.add)
            dve.wait_ge(rows_s, 48)
            for c in range(C):
                last = v.tensor_scalar(m.bin_b[:, c, :], m.ones_f[:, :], m.bin_c[:, c:c + 1], None, ALU.mult)
            last.then_inc(bin_s, 1)
            link(v.tensor_copy(m.bo_parts[0:1, 0, :], m.bo_row[0:1, :]))
            link(v.tensor_tensor(m.bo_rest[0:1, 0, :], m.bo_row[0:1, :], m.bo_parts[0:1, 0, :], ALU.subtract))
            link(v.tensor_copy(m.bo_parts[0:1, 1, :], m.bo_rest[0:1, 0, :]))
            link(v.tensor_tensor(m.bo_rest[0:1, 1, :], m.bo_rest[0:1, 0, :], m.bo_parts[0:1, 1, :],
                                 ALU.subtract))
            v.tensor_copy(m.bo_parts[0:1, 2, :], m.bo_rest[0:1, 1, :]).then_inc(parts_s, 1)
            dve.wait_ge(edges_s, 16 * edge_loads)
            v.tensor_copy(m.tgt_f[:, :], m.tgt_i[:, :])
            v.tensor_scalar(m.e_tmp[:, :], m.tgt_i[:, :], 9, 2, ALU.logical_shift_right, ALU.logical_shift_left)
            link(v.tensor_scalar(m.e_tmp2[:, :], m.tgt_i[:, :], 3, None, ALU.bitwise_and))
            link(v.tensor_tensor(m.bucket_f[:, :], m.e_tmp[:, :], m.e_tmp2[:, :], ALU.add))
            link(v.tensor_scalar(m.e_tmp[:, :], m.tgt_i[:, :], 2, P - 1, ALU.logical_shift_right, ALU.bitwise_and))
            link(v.tensor_copy(m.lo_f[:, :], m.e_tmp[:, :]))
            v.tensor_scalar(m.lo1_f[:, :], m.lo_f[:, :], 1.0, 65536.0, ALU.add, ALU.mult)
            link(v.tensor_scalar(m.e_tmp2[:, :], m.src_i[:, :], 255, None, ALU.bitwise_and))
            link(v.tensor_copy(m.src_lo_f[:, :], m.e_tmp2[:, :]))
            link(v.tensor_scalar(m.e_tmp[:, :], m.src_i[:, :], 8, None, ALU.logical_shift_right))
            link(v.tensor_scalar(m.src_hi_f[:, :], m.e_tmp[:, :], 256.0, None, ALU.mult))
            for l in range(1, LAYERS + 1):
                dve.wait_ge(act_s, l)
                v.tensor_tensor(m.w_lo[l][:, :, :], m.w_f[l][:, :, :], m.w_hi[l][:, :, :].bitcast(F32), ALU.subtract)
            dve.wait_ge(pe_s, 1)
            v.tensor_copy(m.winT[:, :, :].rearrange("p c n -> p (c n)"), m.ps[:, 0, :]).then_inc(win_t_s, 1)
            dve.wait_ge(act_s, LAYERS + 1)
            v.tensor_tensor(m.w_lo[0][:, :, :], m.ps[:, 1:3, :], m.w_hi[0][:, :, :].bitcast(F32), ALU.subtract)
            dve.wait_ge(pe_s, 3)
            link(v.tensor_copy(m.bias0[:, :], m.ps[:, 3, :]))
            v.tensor_tensor(m.bias0[:, 0:D], m.bias0[:, 0:D], m.ps[:, 4, 0:D], ALU.add)
            for l in (1, 2):
                for t in range(2):
                    v.tensor_copy(m.bias_p[l][:, t, :], m.ps[:, 4 + l // 2, (l % 2) * D:(l % 2) * D + D])

        @block.tensor
        def _(pe):
            t = nc.tensor
            pe.wait_ge(w_in_s, 16 * (2 + 2 * LAYERS))
            pe.wait_ge(const_s, 11)
            for h in range(C):
                for c in range(C):
                    last = t.transpose(m.ps[:, 0, h * D + c * P:h * D + (c + 1) * P],
                                       m.win_f[:, c, h * P:(h + 1) * P], m.ident[:, :])
            last.then_inc(pe_s, 1)
            pe.wait_ge(win_t_s, 1)
            for c in range(C):
                for h in range(C):
                    last = t.matmul(m.ps[:, 1 + c, :], m.winT[:, h, c * P:(c + 1) * P], m.w_f[0][:, h, :],
                                    start=h == 0, stop=h == C - 1)
            last.then_inc(pe_s, 1)
            pe.wait_ge(bin_s, 1)
            for h in range(C):
                t.matmul(m.ps[:, 3, :], m.bin_b[:, h, :], m.w_f[0][:, h, :], start=h == 0, stop=h == C - 1)
            pe.wait_ge(rows_s, 48)
            t.matmul(m.ps[:, 4, :], m.ones_f[0:1, :], m.brows[0:1, 0:2 * D], start=True, stop=True)
            t.matmul(m.ps[:, 5, 0:D], m.ones_f[0:1, :], m.brows[0:1, 2 * D:3 * D],
                     start=True, stop=True).then_inc(pe_s, 1)


def split_products(nc, m, out_ap, slot, tile, layer, start=True):
    n = 0
    for c in range(C):
        for h, w in ((m.hT_hi, m.w_hi), (m.hT_hi, m.w_lo), (m.hT_lo, m.w_hi)):
            last = nc.tensor.matmul(out_ap, h[:, slot, tile, c, :], w[layer][:, c, :],
                                    start=start and n == 0, stop=n == 3 * C - 1)
            n += 1
    return last


def first_pass_and_buckets(nc, m):
    NT, NI, EK = m.NT, m.NI, m.EK
    RANK, DEG, SLOT, HT, O = 0, 1, 2, 3, 5
    with ExitStack() as ctx:
        def sem(name):
            return ctx.enter_context(nc.semaphore("p0_" + name))

        x_in = [sem(f"x_in{q}") for q in range(2)]
        stored = [sem(f"stored{q}") for q in range(2)]
        transposed, hi_done, lo_done = sem("transposed"), sem("hi_done"), sem("lo_done")
        multiplied, p_evacuated, t_evacuated = sem("multiplied"), sem("p_evacuated"), sem("t_evacuated")
        t_biased, issue = sem("t_biased"), sem("issue")
        onehot_done, ranked = sem("onehot_done"), sem("ranked")
        rank_read, at_slot_done, counted = sem("rank_read"), sem("at_slot_done"), sem("counted")
        block = ctx.enter_context(nc.Block())

        @block.sync
        def _(sp):
            def load(g, q):
                sp.dma_start(m.in_buf[:, q, :], group_of(m.x, g)).then_inc(x_in[q], 16)

            def body(i):
                for q in range(2):
                    g = 2 * i + q
                    wait(sp, transposed, TPG * g + TPG)
                    if isinstance(i, int) and i == NI - 2 and q == 1:
                        sp.dma_start(m.in_buf[0:m.LASTP, q, :], last_group_of(m, m.x)).then_inc(x_in[q], 16)
                    elif not (isinstance(i, int) and i == NI - 1):
                        load(g + 2, q)
                    wait(sp, p_evacuated, TPG * g + TPG)
                    sp.dma_start(group_of(m.p_tab[0], g), m.p_out[:, q, :]).then_inc(stored[q], 16)
                    wait(sp, t_biased, TPG * g + TPG)
                    sp.dma_start(group_of(m.t_tab[0], g), m.t_out[:, q, :]).then_inc(stored[q], 16)

            load(0, 0)
            load(1, 1)
            body(0)
            if NI > 3:
                with sp.Fori(1, NI - 2) as i:
                    body(i)
            body(NI - 2)
            body(NI - 1)
            for q in range(2):
                sp.wait_ge(stored[q], 32 * NI)

        @block.scalar
        def _(act):
            def split_hi(t, r):
                wait(act, transposed, t + 1)
                wait(act, multiplied, t - 3)
                nc.scalar.activation(m.hT_hi[:, (r // 2) % 2, r % 2, :, :],
                                     m.ps[:, HT + r % 2, 0:D], ACT.Copy).then_inc(hi_done, 1)

            def evacuate_t(t, j):
                wait(act, multiplied, t + 1)
                wait(act, t_biased, t - 3)
                nc.scalar.activation(m.t_raw[:, j % 4, :], m.ps[:, O + j % 2, D:WIDE],
                                     ACT.Copy).then_inc(t_evacuated, 1)

            def body(i):
                for j in range(8):
                    if not (isinstance(i, int) and i == NI - 1 and j == 7):
                        split_hi(8 * i + j + 1, j + 1)
                    evacuate_t(8 * i + j, j)

            split_hi(0, 0)
            run_iterations(act, NI, body)

        @block.gpsimd
        def _(pool):
            def body(i):
                for j in range(8):
                    q = j // TPG
                    c = (j % TPG) * D
                    if j % TPG == 0 and not (isinstance(i, int) and i == 0):
                        wait(pool, stored[q], 32 * i)
                        pool.sem_inc(issue, 1)
                    wait(pool, t_evacuated, 8 * i + j + 1)
                    nc.gpsimd.tensor_tensor(m.t_out[:, q, c:c + D], m.t_raw[:, j % 4, :], m.bias0[:, D:WIDE],
                                            ALU.add).then_inc(t_biased, 1)

            run_iterations(pool, NI, body)

        @block.vector
        def _(dve):
            v = nc.vector

            def split_lo(t, r):
                wait(dve, hi_done, t + 1)
                wait(dve, multiplied, t - 3)
                hi = m.hT_hi[:, (r // 2) % 2, r % 2, :, :].rearrange("p c n -> p (c n)").bitcast(F32)
                v.tensor_tensor(m.hT_lo[:, (r // 2) % 2, r % 2, :, :].rearrange("p c n -> p (c n)"),
                                m.ps[:, HT + r % 2, 0:D], hi, ALU.subtract).then_inc(lo_done, 1)

            def onehots(k, q):
                wait(dve, counted, k - 1)
                v.tensor_scalar(m.oh_bucket[:, q, :], m.iota_h[:, :], m.bucket_f[:, bass.ds(k, 1)], None,
                                ALU.is_equal)
                v.tensor_scalar(m.oh_lo[:, q, :], m.iota_f[:, :], m.lo_f[:, bass.ds(k, 1)], None,
                                ALU.is_equal).then_inc(onehot_done, 1)

            def slots(k, q):
                wait(dve, ranked, k + 1)
                v.tensor_tensor_reduce(out=m.junk[:, :], in0=m.ps[:, RANK, 0:NT], in1=m.oh_bucket[:, q, :],
                                       scale=1.0, scalar=0.0, op0=ALU.mult, op1=ALU.add,
                                       accum_out=m.rank[:, q:q + 1]).then_inc(rank_read, 1)
                wait(dve, rank_read, k + 1)
                for n, number in enumerate((m.lo1_f, m.src_lo_f, m.src_hi_f)):
                    last = v.tensor_scalar(m.at_slot[:, q, n, :], m.iota_f[:, :], m.rank[:, q:q + 1],
                                           number[:, bass.ds(k, 1)], ALU.is_equal, ALU.mult)
                last.then_inc(at_slot_done, 1)

            def evacuate_p(t, i, j):
                q = j // TPG
                wait(dve, t_evacuated, t + 1)
                if j % TPG == 0:
                    wait(dve, stored[q], 32 * i)
                c = (j % TPG) * D
                v.tensor_tensor(m.p_out[:, q, c:c + D], m.ps[:, O + j % 2, 0:D], m.bias0[:, 0:D],
                                ALU.add).then_inc(p_evacuated, 1)

            def body(i):
                final = isinstance(i, int) and i == NI - 1
                for j in range(8):
                    t = 8 * i + j
                    k = 4 * i + j // 2
                    if not (final and j == 7):
                        split_lo(t + 1, j + 1)
                    if j % 2 == 0:
                        slots(k, (j // 2) % 2)
                    elif not (final and j == 7):
                        onehots(k + 1, (j // 2 + 1) % 2)
                    evacuate_p(t, i, j)

            onehots(0, 0)
            split_lo(0, 0)
            run_iterations(dve, NI, body)

        @block.tensor
        def _(pe):
            def transposes(t, i, r):
                if r % TPG == 0:
                    wait(pe, x_in[(r // TPG) % 2], 16 * i + 16)
                wait(pe, hi_done, t - 1)
                wait(pe, lo_done, t - 1)
                src = m.in_buf[:, (r // TPG) % 2, (r % TPG) * D:(r % TPG) * D + D]
                for c in range(C):
                    last = nc.tensor.transpose(m.ps[:, HT + r % 2, c * P:(c + 1) * P],
                                               src[:, c * P:(c + 1) * P], m.ident[:, :])
                last.then_inc(transposed, 1)

            def counts(bank, lhs, q):
                return nc.tensor.matmul(m.ps[:, bank, 0:NT], lhs, m.oh_bucket[:, q, :], start=False, stop=True,
                                        skip_group_check=True)

            def body(i):
                final = isinstance(i, int) and i == NI - 1
                for j in range(8):
                    t = 8 * i + j
                    k = 4 * i + j // 2
                    q = (j // 2) % 2
                    if j % 2 == 0:
                        wait(pe, onehot_done, k + 1)
                        counts(RANK, m.before[:, :], q).then_inc(ranked, 1)
                    if not (final and j == 7):
                        transposes(t + 1, i + (j + 1) // 8, (j + 1) % 8)
                    wait(pe, hi_done, t + 1)
                    wait(pe, lo_done, t + 1)
                    wait(pe, p_evacuated, t - 1)
                    split_products(nc, m, m.ps[:, O + j % 2, :], (j // 2) % 2, j % 2, 0).then_inc(multiplied, 1)
                    if j % 2 == 1:
                        wait(pe, at_slot_done, k + 1)
                        counts(RANK, m.notbefore[:, :], q)
                        counts(DEG, m.oh_lo[:, q, :], q)
                        for n in range(3):
                            last = counts(SLOT, m.at_slot[:, q, n, :], q)
                        last.then_inc(counted, 1)

            for bank in (RANK, DEG, SLOT):
                nc.tensor.matmul(m.ps[:, bank, 0:NT], m.zeros_b[:, 0:P], m.zeros_b[:, 0:NT], start=True, stop=True,
                                 skip_group_check=True)
            transposes(0, 0, 0)
            run_iterations(pe, NI, body)


def finish_tables(nc, m):
    RANK, DEG, SLOT = 0, 1, 2
    NT = m.NT
    with ExitStack() as ctx:
        dve_s = ctx.enter_context(nc.semaphore("tab_dve"))
        block = ctx.enter_context(nc.Block())

        @block.vector
        def _(dve):
            v = nc.vector
            chain = [0]

            def link(ins):
                chain[0] += 1
                ins.then_inc(dve_s, 1)
                dve.wait_ge(dve_s, chain[0])

            link(v.tensor_scalar(m.tab_a[:, :], m.ps[:, DEG, 0:NT], 1.0, None, ALU.max))
            v.reciprocal(m.inv_deg[:, :], m.tab_a[:, :])
            link(v.tensor_scalar(m.full_m[:, :], m.ps[:, RANK, 0:NT], float(P), None, ALU.is_gt))
            link(v.reduce_max(m.flag_f[:, :], m.full_m[:, :], mybir.AxisListType.X))
            link(v.tensor_copy(m.flag_i[:, :], m.flag_f[:, :]))
            link(v.tensor_copy(m.slot_i[:, :], m.ps[:, SLOT, 0:NT]))
            link(v.tensor_scalar(m.slot_src[:, :], m.slot_i[:, :], 16, None, ALU.logical_shift_right))
            link(v.tensor_copy(m.slot_lo[:, :], m.slot_src[:, :]))
            link(v.tensor_scalar(m.slot_lo[:, :], m.slot_lo[:, :], -1.0, None, ALU.add))
            link(v.tensor_scalar(m.slot_i[:, :], m.slot_i[:, :], 65535, None, ALU.bitwise_and))
            link(v.tensor_copy(m.tab_a[:, :], m.slot_i[:, :]))
            link(v.tensor_scalar(m.tab_b[:, :], m.slot_lo[:, :], 0.0, float(FAR), ALU.is_lt, ALU.mult))
            link(v.tensor_tensor(m.tab_a[:, :], m.tab_a[:, :], m.tab_b[:, :], ALU.add))
            link(v.tensor_scalar(m.tab_b[:, :], m.full_m[:, :], float(FAR), None, ALU.mult))
            link(v.tensor_tensor(m.tab_a[:, :], m.tab_a[:, :], m.tab_b[:, :], ALU.add))
            link(v.tensor_copy(m.slot_src[:, :], m.tab_a[:, :]))
            link(v.tensor_scalar(m.tab_b[:, :], m.full_m[:, :], float(-P), None, ALU.mult))
            link(v.tensor_tensor(m.slot_lo[:, :], m.slot_lo[:, :], m.tab_b[:, :], ALU.add))


def add_overfull_buckets(nc, m, layer):
    EK, NT, NROW = m.EK, m.NT, m.NROW
    TARGETS, SUMS, LO_T, WEIGHTS = 0, 1, 2, 3
    NEW, OLD = 0, 1
    STEPS = 8
    with ExitStack() as ctx:
        def sem(name):
            return ctx.enter_context(nc.semaphore(f"over{layer}_{name}"))

        turn, issue = sem("turn"), sem("issue")
        spread_done, targets_done, same_done = sem("spread_done"), sem("targets_done"), sem("same_done")
        weights_done, index_done = sem("weights_done"), sem("index_done")
        rows_in, old_in, written = sem("rows_in"), sem("old_in"), sem("written")
        summed, added, dve_s = sem("summed"), sem("added"), sem("dve")
        block = ctx.enter_context(nc.Block())

        def if_overfull(engine):
            flag = engine.value_load(m.flag_i[0:1, 0:1], min_val=0, max_val=1)
            return engine.If(flag)

        @block.gpsimd
        def _(pool):
            def indexed(out, out_offset, in_, in_offset, sem_):
                nc.gpsimd.indirect_dma_start(out=out, out_offset=out_offset, in_=in_, in_offset=in_offset,
                                             bounds_check=NROW - 1, oob_is_err=False).then_inc(sem_, 16)

            with if_overfull(pool):
                pool.sem_inc(turn, 1)
                with pool.Fori(0, EK) as k:
                    pool.wait_ge(spread_done, k + 1)
                    pool.sem_inc(issue, 1)
                    indexed(m.gath[:, NEW, :], None, m.t_tab[layer][:, :],
                            bass.IndirectOffsetOnAxis(ap=m.over_src[:, :], axis=0), rows_in)
                    pool.wait_ge(index_done, k + 1)
                    pool.sem_inc(issue, 1)
                    indexed(m.gath[:, OLD, :], None, m.p_tab[layer][:, :],
                            bass.IndirectOffsetOnAxis(ap=m.over_row[:, :], axis=0), old_in)
                    pool.wait_ge(added, k + 1)
                    pool.sem_inc(issue, 1)
                    indexed(m.p_tab[layer][:, :], bass.IndirectOffsetOnAxis(ap=m.over_row[:, :], axis=0),
                            m.v_buf[:, 0, 0, :], None, written)
                    pool.wait_ge(written, 16 * k + 16)
                    pool.sem_inc(turn, 1)

        @block.vector
        def _(dve):
            v = nc.vector
            with if_overfull(dve):
                with dve.Fori(0, EK) as k:
                    n = [0]

                    def link(ins):
                        n[0] += 1
                        ins.then_inc(dve_s, 1)
                        dve.wait_ge(dve_s, STEPS * k + n[0])

                    column = bass.ds(k, 1)
                    dve.wait_ge(turn, k + 1)
                    v.tensor_copy(m.over_src[:, :], m.src_i[:, column])
                    v.tensor_scalar(m.over_bucket[:, :], m.iota_h[:, :], m.bucket_f[:, column], None, ALU.is_equal)
                    v.tensor_scalar(m.over_lo[:, :], m.iota_f[:, :], m.lo_f[:, column], None, ALU.is_equal)
                    v.tensor_scalar(m.over_spread[:, :], m.ones_f[:, :], m.tgt_f[:, column], None,
                                    ALU.mult).then_inc(spread_done, 1)
                    dve.wait_ge(targets_done, k + 1)
                    v.tensor_copy(m.over_loT[:, :], m.ps[:, LO_T, 0:P])
                    v.tensor_scalar(m.over_same[:, :], m.ps[:, TARGETS, 0:P], m.tgt_f[:, column], None,
                                    ALU.is_equal).then_inc(same_done, 1)
                    dve.wait_ge(same_done, k + 1)
                    link(v.tensor_tensor_reduce(out=m.over_earlier[:, :], in0=m.over_same[:, :],
                                                in1=m.after_f[:, :], scale=1.0, scalar=0.0, op0=ALU.mult,
                                                op1=ALU.add, accum_out=m.over_n[:, 0:1]))
                    link(v.tensor_tensor_reduce(out=m.junk[:, :], in0=m.over_bucket[:, :], in1=m.full_m[:, :],
                                                scale=1.0, scalar=0.0, op0=ALU.mult, op1=ALU.add,
                                                accum_out=m.over_n[:, 1:2]))
                    link(v.tensor_scalar(m.over_n[:, 2:3], m.over_n[:, 0:1], 0.0, float(FAR), ALU.is_gt, ALU.mult))
                    link(v.tensor_scalar(m.over_n[:, 3:4], m.over_n[:, 1:2], float(-FAR), float(FAR), ALU.mult,
                                         ALU.add))
                    link(v.tensor_tensor(m.over_n[:, 2:3], m.over_n[:, 2:3], m.over_n[:, 3:4], ALU.add))
                    link(v.tensor_tensor(m.over_n[:, 2:3], m.over_n[:, 2:3], m.tgt_f[:, column], ALU.add))
                    v.tensor_copy(m.over_row[:, :], m.over_n[:, 2:3]).then_inc(index_done, 1)
                    dve.wait_ge(weights_done, k + 1)
                    link(v.tensor_tensor_reduce(out=m.junk[:, :], in0=m.ps[:, WEIGHTS, 0:NT],
                                                in1=m.over_bucket[:, :], scale=1.0, scalar=0.0, op0=ALU.mult,
                                                op1=ALU.add, accum_out=m.over_n[:, 4:5]))
                    dve.wait_ge(summed, k + 1)
                    dve.wait_ge(old_in, 16 * k + 16)
                    link(v.tensor_scalar(m.v_buf[:, 0, 1, :], m.ps[:, SUMS, 0:D], m.over_n[:, 4:5], None, ALU.mult))
                    v.tensor_tensor(m.v_buf[:, 0, 0, :], m.v_buf[:, 0, 1, :], m.gath[:, OLD, :],
                                    ALU.add).then_inc(added, 1)
                    assert n[0] == STEPS

        @block.tensor
        def _(pe):
            with if_overfull(pe):
                with pe.Fori(0, EK) as k:
                    pe.wait_ge(spread_done, k + 1)
                    nc.tensor.matmul(m.ps[:, TARGETS, 0:P], m.over_spread[:, :], m.ident[:, :],
                                     start=True, stop=True)
                    nc.tensor.transpose(m.ps[:, LO_T, 0:P], m.over_lo[:, :], m.ident[:, :]).then_inc(targets_done, 1)
                    pe.wait_ge(same_done, k + 1)
                    nc.tensor.matmul(m.ps[:, WEIGHTS, 0:NT], m.over_loT[:, :], m.inv_deg[:, :],
                                     start=True, stop=True).then_inc(weights_done, 1)
                    pe.wait_ge(rows_in, 16 * k + 16)
                    nc.tensor.matmul(m.ps[:, SUMS, 0:D], m.over_same[:, :], m.gath[:, NEW, :],
                                     start=True, stop=True).then_inc(summed, 1)


class GatheringPass:

    def __init__(self, nc, m, layer, sem):
        self.nc, self.m, self.layer = nc, m, layer
        self.p_in = [sem(f"p_in{q}") for q in range(2)]
        self.gathered = [sem(f"gathered{r}") for r in range(8)]
        self.index_done = sem("index_done")
        self.issue = sem("issue")
        self.gath_hi_done, self.gath_lo_done = sem("gath_hi_done"), sem("gath_lo_done")
        self.picked, self.summed, self.v_done = sem("picked"), sem("summed"), sem("v_done")
        self.transposed, self.hi_done, self.lo_done = sem("transposed"), sem("hi_done"), sem("lo_done")
        self.multiplied = sem("multiplied")

    def at(self, i, j, ahead):
        u = 4 * i + j + ahead
        if isinstance(u, int) and not 0 <= u < 4 * self.m.NI:
            return None
        return u, i + (j + ahead) // 4, (j + ahead) % 4

    def run(self, engine, step, flush=0):
        NI = self.m.NI
        for j in range(1, 4):
            step(-1, j)

        def body(i):
            for j in range(4):
                step(i, j)

        run_iterations(engine, NI, body)
        for j in range(flush):
            step(NI, j)

    def gather_program(self, pool, used):
        m, nc = self.m, self.nc

        def body(i):
            for h in range(2):
                if not (isinstance(i, int) and i == 0):
                    wait(pool, used, 4 * i + 2 * h - 2)
                    pool.sem_inc(self.issue, 1)
                nc.gpsimd.tensor_copy(m.idx8[:, h, 0:4],
                                      m.slot_src[:, bass.ds(8 * i + 4 * h, 4)]).then_inc(self.index_done, 1)
                wait(pool, self.index_done, 2 * i + h + 1)
                pool.sem_inc(self.issue, 1)
                for n in range(4):
                    nc.gpsimd.indirect_dma_start(
                        out=m.gath[:, 4 * h + n, :], out_offset=None, in_=m.t_tab[self.layer - 1][:, :],
                        in_offset=bass.IndirectOffsetOnAxis(ap=m.idx8[:, h, n:n + 1], axis=0),
                        bounds_check=m.NROW - 1, oob_is_err=False).then_inc(self.gathered[4 * h + n], 16)

        run_iterations(pool, m.NI, body)

    def split_hi(self, act, i, j):
        m = self.m
        if place := self.at(i, j, 1):
            u, _, r = place
            wait(act, self.transposed, u + 1)
            wait(act, self.multiplied, u - 1)
            self.nc.scalar.activation(m.hT_hi[:, r % 2, :, :, :].rearrange("p t c n -> p (t c n)"),
                                      m.ps[:, 2 + r % 2, :], ACT.Relu).then_inc(self.hi_done, 1)

    def split_gathered_hi(self, act, i, j):
        m = self.m
        if place := self.at(i, j, 3):
            u, n, r = place
            for q in (2 * r, 2 * r + 1):
                wait(act, self.gathered[q], 16 * n + 16)
            wait(act, self.summed, u - 1)
            wait(act, self.gath_lo_done, u - 1)
            self.nc.scalar.activation(m.gath_hi[:, r % 2, :, :], m.gath[:, 2 * r:2 * r + 2, :],
                                      ACT.Copy).then_inc(self.gath_hi_done, 1)

    def split_lo(self, dve, i, j):
        m = self.m
        if place := self.at(i, j, 1):
            u, _, r = place
            wait(dve, self.hi_done, u + 1)
            self.nc.vector.scalar_tensor_tensor(
                out=m.hT_lo[:, r % 2, :, :, :].rearrange("p t c n -> p (t c n)"), in0=m.ps[:, 2 + r % 2, :],
                scalar=0.0, in1=m.hT_hi[:, r % 2, :, :, :].rearrange("p t c n -> p (t c n)").bitcast(F32),
                op0=ALU.max, op1=ALU.subtract).then_inc(self.lo_done, 1)

    def make_v(self, dve, i, j, between=lambda: None):
        m = self.m
        if place := self.at(i, j, 2):
            u, n, r = place
            if r % 2 == 0:
                wait(dve, self.p_in[r // 2], 16 * n + 16)
            wait(dve, self.summed, u + 1)
            wait(dve, self.transposed, u - 1)
            for t in range(2):
                c = (2 * (r % 2) + t) * D
                last = self.nc.vector.scalar_tensor_tensor(
                    out=m.v_buf[:, r % 2, t, :], in0=m.ps[:, r % 2, t * D:(t + 1) * D],
                    scalar=m.inv_deg[:, bass.ds(2 * u + t, 1)], in1=m.in_buf[:, r // 2, c:c + D],
                    op0=ALU.mult, op1=ALU.add)
                if t == 0:
                    between()
            last.then_inc(self.v_done, 1)
        else:
            between()

    def split_gathered_lo(self, dve, i, j):
        m = self.m
        if place := self.at(i, j, 3):
            u, _, r = place
            wait(dve, self.gath_hi_done, u + 1)
            self.nc.vector.tensor_tensor(m.gath_lo[:, r % 2, :, :], m.gath[:, 2 * r:2 * r + 2, :],
                                         m.gath_hi[:, r % 2, :, :].bitcast(F32),
                                         ALU.subtract).then_inc(self.gath_lo_done, 1)

    def make_pick(self, dve, i, j, pick):
        m = self.m
        if place := self.at(i, j, 3):
            u, _, r = place
            wait(dve, self.summed, u - 1)
            for t in range(2):
                last = self.nc.vector.tensor_scalar(pick[:, r % 2, t, :], m.iota_f[:, :],
                                                    m.slot_lo[:, bass.ds(2 * u + t, 1)], None, ALU.is_equal)
            last.then_inc(self.picked, 1)

    def sum_per_node(self, pe, i, j):
        m = self.m
        if place := self.at(i, j, 2):
            u, _, r = place
            wait(pe, self.gath_lo_done, u + 1)
            wait(pe, self.picked, u + 1)
            wait(pe, self.v_done, u - 1)
            for t in range(2):
                for n, rows in enumerate((m.gath_hi, m.gath_lo)):
                    last = self.nc.tensor.matmul(m.ps[:, r % 2, t * D:(t + 1) * D], m.pick[:, r % 2, t, :],
                                                 rows[:, r % 2, t, :], start=n == 0, stop=n == 1)
            last.then_inc(self.summed, 1)

    def sum_per_node_unsplit(self, pe, i, j):
        m = self.m
        if place := self.at(i, j, 2):
            u, n, r = place
            for q in (2 * r, 2 * r + 1):
                wait(pe, self.gathered[q], 16 * n + 16)
            wait(pe, self.picked, u + 1)
            wait(pe, self.v_done, u - 1)
            for t in range(2):
                last = self.nc.tensor.matmul(m.ps[:, r % 2, t * D:(t + 1) * D], m.pick_f[:, r % 2, t, :],
                                             m.gath[:, 2 * r + t, :], start=True, stop=True)
            last.then_inc(self.summed, 1)

    def transpose_v(self, pe, i, j):
        m = self.m
        if place := self.at(i, j, 1):
            u, _, r = place
            wait(pe, self.v_done, u + 1)
            wait(pe, self.lo_done, u - 1)
            for t in range(2):
                for c in range(C):
                    last = self.nc.tensor.transpose(m.ps[:, 2 + r % 2, (2 * t + c) * P:(2 * t + c + 1) * P],
                                                    m.v_buf[:, r % 2, t, c * P:(c + 1) * P], m.ident[:, :])
            last.then_inc(self.transposed, 1)


def middle_pass(nc, m, layer):
    NI = m.NI
    with ExitStack() as ctx:
        def sem(name):
            return ctx.enter_context(nc.semaphore(f"p{layer}_{name}"))

        g = GatheringPass(nc, m, layer, sem)
        stored = [sem(f"stored{q}") for q in range(2)]
        p_evacuated, t_evacuated = sem("p_evacuated"), sem("t_evacuated")
        block = ctx.enter_context(nc.Block())

        @block.sync
        def _(sp):
            def load(group, q):
                sp.dma_start(m.in_buf[:, q, :], group_of(m.p_tab[layer - 1], group)).then_inc(g.p_in[q], 16)

            def body(i):
                for q in range(2):
                    group = 2 * i + q
                    if not (isinstance(i, int) and i == NI - 1):
                        wait(sp, g.v_done, 2 * group + 2)
                        load(group + 2, q)
                    wait(sp, p_evacuated, 2 * group + 2)
                    sp.dma_start(group_of(m.p_tab[layer], group), m.p_out[:, q, :]).then_inc(stored[q], 16)
                    wait(sp, t_evacuated, 2 * group + 2)
                    sp.dma_start(m.t_tab[layer][bass.ds(group * GROUP, GROUP), :]
                                 .rearrange("(p j) d -> p (j d)", j=TPG), m.t_out[:, q, :]).then_inc(stored[q], 16)

            load(0, 0)
            load(1, 1)
            run_iterations(sp, NI, body)
            for q in range(2):
                sp.wait_ge(stored[q], 32 * NI)

        @block.gpsimd
        def _(pool):
            g.gather_program(pool, g.gath_lo_done)

        @block.scalar
        def _(act):
            def evacuate_t(i, j):
                if place := g.at(i, j, 0):
                    u, n, r = place
                    wait(act, g.multiplied, u + 1)
                    if r % 2 == 0:
                        wait(act, stored[r // 2], 32 * n)
                    nc.scalar.activation(
                        m.t_out[:, r // 2, (r % 2) * WIDE:(r % 2 + 1) * WIDE].rearrange("p (t d) -> p t d", t=2),
                        m.ps[:, 4 + 2 * (r % 2):6 + 2 * (r % 2), D:WIDE], ACT.Copy).then_inc(t_evacuated, 1)

            def step(i, j):
                g.split_gathered_hi(act, i, j)
                g.split_hi(act, i, j)
                evacuate_t(i, j)

            g.run(act, step)

        @block.vector
        def _(dve):
            def evacuate_p(i, j):
                if place := g.at(i, j, 0):
                    u, n, r = place
                    wait(dve, t_evacuated, u + 1)
                    if r % 2 == 0:
                        wait(dve, stored[r // 2], 32 * n)
                    nc.vector.tensor_tensor(
                        m.p_out[:, r // 2, (r % 2) * WIDE:(r % 2 + 1) * WIDE].rearrange("p (t d) -> p t d", t=2),
                        m.ps[:, 4 + 2 * (r % 2):6 + 2 * (r % 2), 0:D], m.bias_p[layer][:, :, :],
                        ALU.add).then_inc(p_evacuated, 1)

            def step(i, j):
                g.split_gathered_lo(dve, i, j)
                g.make_pick(dve, i, j, m.pick)
                g.make_v(dve, i, j)
                g.split_lo(dve, i, j)
                evacuate_p(i, j)

            g.run(dve, step)

        @block.tensor
        def _(pe):
            def multiply(i, j):
                if place := g.at(i, j, 0):
                    u, _, r = place
                    wait(pe, g.lo_done, u + 1)
                    wait(pe, p_evacuated, u - 1)
                    for t in range(2):
                        last = split_products(nc, m, m.ps[:, 4 + 2 * (r % 2) + t, :], r % 2, t, layer)
                    last.then_inc(g.multiplied, 1)

            def step(i, j):
                g.sum_per_node(pe, i, j)
                g.transpose_v(pe, i, j)
                multiply(i, j)

            g.run(pe, step)


def last_pass(nc, m):
    NI = m.NI
    with ExitStack() as ctx:
        def sem(name):
            return ctx.enter_context(nc.semaphore(f"p{LAYERS}_{name}"))

        g = GatheringPass(nc, m, LAYERS, sem)
        x_in = [sem(f"x_in{q}") for q in range(2)]
        stored = [sem(f"stored{q}") for q in range(2)]
        y_done, mean_done, squared = sem("y_done"), sem("mean_done"), sem("squared")
        var_done, root_done, scale_done = sem("var_done"), sem("root_done"), sem("scale_done")
        normed, dve_s = sem("normed"), sem("dve")
        block = ctx.enter_context(nc.Block())

        @block.sync
        def _(sp):
            def load_p(group, q):
                sp.dma_start(m.in_buf[:, q, :], group_of(m.p_tab[LAYERS - 1], group)).then_inc(g.p_in[q], 16)

            def load_x(group, q, last):
                if last:
                    sp.dma_start(m.x_buf[0:m.LASTP, q, :], last_group_of(m, m.x)).then_inc(x_in[q], 16)
                else:
                    sp.dma_start(m.x_buf[:, q, :], group_of(m.x, group)).then_inc(x_in[q], 16)

            def body(i):
                for q in range(2):
                    group = 2 * i + q
                    if not (isinstance(i, int) and i == NI - 1):
                        wait(sp, g.v_done, 2 * group + 2)
                        load_p(group + 2, q)
                        wait(sp, y_done, 2 * group + 2)
                        load_x(group + 2, q, isinstance(i, int) and i == NI - 2 and q == 1)
                    if not (isinstance(i, int) and i == 0 and q == 0):
                        wait(sp, normed, 2 * group)
                        sp.dma_start(group_of(m.out, group - 1), m.p_out[:, 1 - q, :]).then_inc(stored[1 - q], 16)

            for q in range(2):
                load_p(q, q)
                load_x(q, q, False)
            body(0)
            if NI > 3:
                with sp.Fori(1, NI - 2) as i:
                    body(i)
            body(NI - 2)
            body(NI - 1)
            sp.wait_ge(normed, 4 * NI)
            sp.dma_start(last_group_of(m, m.out), m.p_out[0:m.LASTP, 1, :]).then_inc(stored[1], 16)
            for q in range(2):
                sp.wait_ge(stored[q], 16 * NI)

        @block.gpsimd
        def _(pool):
            g.gather_program(pool, g.summed)

        @block.scalar
        def _(act):
            def square(i, j):
                if place := g.at(i, j, -1):
                    u, _, r = place
                    wait(act, mean_done, u + 1)
                    for k in (2 * r, 2 * r + 1):
                        last = nc.scalar.activation(m.square[:, k, :], m.y_buf[:, k, :], ACT.Square,
                                                    bias=m.minus_mean[:, k:k + 1], accum_out=m.squares[:, k:k + 1])
                    last.then_inc(squared, 1)

            def root(i, j):
                if place := g.at(i, j, -2):
                    u, _, r = place
                    wait(act, var_done, u + 1)
                    nc.scalar.activation(m.root[:, 2 * r:2 * r + 2], m.ve[:, 2 * r:2 * r + 2],
                                         ACT.Sqrt).then_inc(root_done, 1)

            def normalise(i, j):
                if place := g.at(i, j, -3):
                    u, n, r = place
                    wait(act, scale_done, u + 1)
                    if r % 2 == 0:
                        wait(act, stored[r // 2], 16 * n)
                    for t in range(2):
                        k = 2 * r + t
                        c = (2 * (r % 2) + t) * D
                        last = nc.scalar.activation(m.p_out[:, r // 2, c:c + D], m.y_buf[:, k, :], ACT.Identity,
                                                    bias=m.shift[:, k:k + 1], scale=m.rstd[:, k:k + 1])
                    last.then_inc(normed, 1)

            def step(i, j):
                g.split_hi(act, i, j)
                square(i, j)
                root(i, j)
                normalise(i, j)

            g.run(act, step, flush=3)

        @block.vector
        def _(dve):
            v = nc.vector

            def residual(i, j):
                if place := g.at(i, j, 0):
                    u, n, r = place
                    wait(dve, g.multiplied, u + 1)
                    if r % 2 == 0:
                        wait(dve, x_in[r // 2], 16 * n + 16)
                    wait(dve, normed, u - 3)
                    for t in range(2):
                        k = 2 * r + t
                        c = (2 * (r % 2) + t) * D
                        last = v.scalar_tensor_tensor(
                            out=m.y_buf[:, k, :], in0=m.ps[:, 4 + r % 2, t * D:(t + 1) * D], scalar=1.0,
                            in1=m.x_buf[:, r // 2, c:c + D], op0=ALU.mult, op1=ALU.add,
                            accum_out=m.y_sum[:, k:k + 1])
                    last.then_inc(y_done, 1)
                    wait(dve, y_done, u + 1)
                    v.tensor_scalar(m.minus_mean[:, 2 * r:2 * r + 2], m.y_sum[:, 2 * r:2 * r + 2], -1.0 / D, None,
                                    ALU.mult).then_inc(mean_done, 1)

            def variance(i, j):
                if place := g.at(i, j, -2):
                    u, _, r = place
                    wait(dve, squared, u + 1)
                    v.tensor_scalar(m.ve[:, 2 * r:2 * r + 2], m.squares[:, 2 * r:2 * r + 2], 1.0 / D, EPS,
                                    ALU.mult, ALU.add).then_inc(var_done, 1)

            def scales(i, j):
                place = g.at(i, j, -3)
                if place is None:
                    return [lambda: None] * 6
                u, _, r = place
                k = slice(2 * r, 2 * r + 2)
                rstd, newton = m.rstd[:, k], m.newton[:, k]

                def invert():
                    wait(dve, root_done, u + 1)
                    v.reciprocal(rstd, m.root[:, k]).then_inc(dve_s, 1)

                def times_ve():
                    wait(dve, dve_s, 5 * u + 1)
                    v.tensor_tensor(newton, rstd, m.ve[:, k], ALU.mult).then_inc(dve_s, 1)

                def times_rstd():
                    wait(dve, dve_s, 5 * u + 2)
                    v.tensor_tensor(newton, newton, rstd, ALU.mult).then_inc(dve_s, 1)

                def factor():
                    wait(dve, dve_s, 5 * u + 3)
                    v.tensor_scalar(newton, newton, -0.5, 1.5, ALU.mult, ALU.add).then_inc(dve_s, 1)

                def improve():
                    wait(dve, dve_s, 5 * u + 4)
                    v.tensor_tensor(rstd, rstd, newton, ALU.mult).then_inc(dve_s, 1)

                def shift():
                    wait(dve, dve_s, 5 * u + 5)
                    v.tensor_tensor(m.shift[:, k], m.minus_mean[:, k], rstd, ALU.mult).then_inc(scale_done, 1)

                return invert, times_ve, times_rstd, factor, improve, shift

            def step(i, j):
                invert, times_ve, times_rstd, factor, improve, shift = scales(i, j)
                invert()
                variance(i, j)
                times_ve()
                g.make_pick(dve, i, j, m.pick_f)
                times_rstd()
                g.make_v(dve, i, j, between=factor)
                improve()
                g.split_lo(dve, i, j)
                shift()
                residual(i, j)

            g.run(dve, step, flush=3)

        @block.tensor
        def _(pe):
            def multiply(i, j):
                if place := g.at(i, j, 0):
                    u, _, r = place
                    wait(pe, g.lo_done, u + 1)
                    wait(pe, y_done, u - 1)
                    for t in range(2):
                        o = m.ps[:, 4 + r % 2, t * D:(t + 1) * D]
                        nc.tensor.matmul(o, m.ones_b[0:3, :], m.bo_3[0:3, :], start=True, stop=False)
                        last = split_products(nc, m, o, r % 2, t, LAYERS, start=False)
                    last.then_inc(g.multiplied, 1)

            def step(i, j):
                g.sum_per_node_unsplit(pe, i, j)
                g.transpose_v(pe, i, j)
                multiply(i, j)

            g.run(pe, step)


def build_program(nc, x, src, dst, w_in, b_in, w_agg, w_self, b_hid, w_out, b_out, out):
    m = Memory()
    N = x.shape[0]
    E = src.shape[0]
    NG = -(-N // GROUP)
    NT = NG * TPG
    NROW = NG * GROUP
    LASTP = (N - (NG - 1) * GROUP) // TPG
    EK = 2 * NG
    EFULL = E // EK
    EREST = E - EFULL * EK
    NI = NG // 2
    assert NG % 2 == 0 and NG >= 6 and E <= EK * P and NT <= 512 and NROW <= 65536
    assert N % TPG == 0 and NROW < FAR

    with ExitStack() as ctx:
        def sb(name, shape, dt):
            return ctx.enter_context(nc.sbuf_tensor(name, shape, dt))

        m.p_tab = [nc.dram_tensor(f"p_tab{l}", [NROW, D], F32, kind="Internal").ap() for l in range(LAYERS)]
        m.t_tab = [nc.dram_tensor(f"t_tab{l}", [NROW, D], F32, kind="Internal").ap() for l in range(LAYERS)]

        m.ident = sb("ident", [P, P], F32)
        m.iota_i = sb("iota_i", [P, max(NT, P)], I32)
        m.iota_f = sb("iota_f", [P, P], F32)
        m.iota_h = sb("iota_h", [P, NT], F16)
        m.before = sb("before", [P, P], BF16)
        m.notbefore = sb("notbefore", [P, P], BF16)
        m.after_f = sb("after_f", [P, P], F32)
        m.zeros_b = sb("zeros_b", [P, 512], BF16)
        m.ones_f = sb("ones_f", [P, P], F32)
        m.ones_b = sb("ones_b", [3, P], BF16)

        m.w_f = [sb(f"w_f{l}", [P, C, WIDE], F32) for l in range(LAYERS)]
        m.w_f.append(sb("wo_f", [P, C, D], F32))
        m.win_f = sb("win_f", [P, C, D], F32)
        m.winT = sb("winT", [P, C, D], F32)
        widths = [WIDE] * LAYERS + [D]
        m.w_hi = [sb(f"w_hi{l}", [P, C, widths[l]], F32R) for l in range(LAYERS + 1)]
        m.w_lo = [sb(f"w_lo{l}", [P, C, widths[l]], F32R) for l in range(LAYERS + 1)]
        m.brows = sb("brows", [1, 2 * D + D], F32)
        m.bo_row = sb("bo_row", [1, D], F32)
        m.bo_rest = sb("bo_rest", [1, 2, D], F32)
        m.bo_parts = sb("bo_parts", [1, 3, D], BF16)
        m.bo_3 = sb("bo_3", [3, D], BF16)
        m.bin_c = sb("bin_c", [P, C], F32)
        m.bin_b = sb("bin_b", [P, C, P], F32)
        m.bias0 = sb("bias0", [P, WIDE], F32)
        m.bias_p = [None] + [sb(f"bias_p{l}", [P, 2, D], F32) for l in (1, 2)]

        m.tgt_i = sb("tgt_i", [P, EK], I32)
        m.src_i = sb("src_i", [P, EK], I32)
        m.e_tmp = sb("e_tmp", [P, EK], I32)
        m.e_tmp2 = sb("e_tmp2", [P, EK], I32)
        m.tgt_f = sb("tgt_f", [P, EK], F32)
        m.bucket_f = sb("bucket_f", [P, EK], F32)
        m.lo_f = sb("lo_f", [P, EK], F32)
        m.lo1_f = sb("lo1_f", [P, EK], F32)
        m.src_lo_f = sb("src_lo_f", [P, EK], F32)
        m.src_hi_f = sb("src_hi_f", [P, EK], F32)
        m.slot_i = sb("slot_i", [P, NT], I32)
        m.slot_lo = sb("slot_lo", [P, NT], F32)
        m.slot_src = sb("slot_src", [P, NT], I32)
        m.inv_deg = sb("inv_deg", [P, NT], F32)
        m.full_m = sb("full_m", [P, NT], F32)
        m.tab_a = sb("tab_a", [P, NT], F32)
        m.tab_b = sb("tab_b", [P, NT], F32)
        m.flag_f = sb("flag_f", [P, 1], F32)
        m.flag_i = sb("flag_i", [P, 1], I32)

        m.in_buf = sb("in_buf", [P, 2, TPG * D], F32)
        m.x_buf = sb("x_buf", [P, 2, TPG * D], F32)
        m.p_out = sb("p_out", [P, 2, TPG * D], F32)
        m.t_raw = sb("t_raw", [P, 4, D], F32)
        m.t_out = sb("t_out", [P, 2, TPG * D], F32)
        m.hT_hi = sb("hT_hi", [P, 2, 2, C, P], F32R)
        m.hT_lo = sb("hT_lo", [P, 2, 2, C, P], F32R)
        m.gath = sb("gath", [P, 8, D], F32)
        m.gath_hi = sb("gath_hi", [P, 2, 2, D], F32R)
        m.gath_lo = sb("gath_lo", [P, 2, 2, D], F32R)
        m.idx8 = sb("idx8", [P, 2, 8], I32)
        m.pick = sb("pick", [P, 2, 2, P], F32R)
        m.v_buf = sb("v_buf", [P, 2, 2, D], F32)
        m.pick_f = sb("pick_f", [P, 2, 2, P], F32)
        m.y_buf = sb("y_buf", [P, 8, D], F32)
        m.square = sb("square", [P, 8, D], BF16)
        m.y_sum = sb("y_sum", [P, 8], F32)
        m.minus_mean = sb("minus_mean", [P, 8], F32)
        m.squares = sb("squares", [P, 8], F32)
        m.ve = sb("ve", [P, 8], F32)
        m.root = sb("root", [P, 8], F32)
        m.newton = sb("newton", [P, 8], F32)
        m.rstd = sb("rstd", [P, 8], F32)
        m.shift = sb("shift", [P, 8], F32)
        m.over_src = sb("over_src", [P, 1], I32)
        m.over_row = sb("over_row", [P, 1], I32)
        m.over_spread = sb("over_spread", [P, P], F32)
        m.over_bucket = sb("over_bucket", [P, NT], F32)
        m.over_lo = sb("over_lo", [P, P], F32)
        m.over_loT = sb("over_loT", [P, P], F32)
        m.over_earlier = sb("over_earlier", [P, P], F32)
        m.over_n = sb("over_n", [P, 5], F32)
        m.over_same = sb("over_same", [P, P], F32)
        m.oh_bucket = sb("oh_bucket", [P, 2, NT], BF16)
        m.oh_lo = sb("oh_lo", [P, 2, P], BF16)
        m.at_slot = sb("at_slot", [P, 2, 3, P], BF16)
        m.rank = sb("rank", [P, 2], F32)
        m.junk = sb("junk", [P, NT], F32)

        m.ps = ctx.enter_context(nc.psum_tensor("ps", [P, 8, 512], F32))

        m.N, m.NG, m.NT, m.NROW, m.LASTP = N, NG, NT, NROW, LASTP
        m.EK, m.EFULL, m.EREST, m.NI = EK, EFULL, EREST, NI
        m.x, m.src, m.dst, m.w_in, m.b_in, m.w_agg, m.w_self = x, src, dst, w_in, b_in, w_agg, w_self
        m.b_hid, m.w_out, m.b_out, m.out = b_hid, w_out, b_out, out

        prepare_constants_and_weights(nc, m)
        first_pass_and_buckets(nc, m)
        finish_tables(nc, m)
        for layer in (1, 2):
            add_overfull_buckets(nc, m, layer - 1)
            middle_pass(nc, m, layer)
        add_overfull_buckets(nc, m, LAYERS - 1)
        last_pass(nc, m)


_INS = ["x", "src", "dst", "L0_gnn_W_in", "L0_gnn_b_in", "L0_gnn_W_agg", "L0_gnn_W_self", "L0_gnn_b_hid",
        "L0_gnn_W_out", "L0_gnn_b_out"]


def kernel(**inputs):
    import concourse.bacc as bacc
    from concourse.bass_utils import run_bass_kernel_spmd

    nc = bacc.Bacc("TRN2", target_bir_lowering=False, num_devices=1)
    arrays, args = {}, []
    for name in _INS:
        a = np.ascontiguousarray(inputs[name])
        arrays[f"in_{name}"] = a
        args.append(nc.dram_tensor(f"in_{name}", a.shape, mybir.dt.from_np(a.dtype), kind="ExternalInput").ap())
    out = nc.dram_tensor("out_0", inputs["x"].shape, F32, kind="ExternalOutput").ap()
    build_program(nc, *args, out)
    result = run_bass_kernel_spmd(nc, [arrays], core_ids=[0])
    return result.results[0]["out_0"]
```

```python
import numpy as np
import concourse.bass as bass
from concourse import mybir
from contextlib import ExitStack

F32 = mybir.dt.float32
F32R = mybir.dt.float32r
BF16 = mybir.dt.bfloat16
F16 = mybir.dt.float16
I32 = mybir.dt.int32
ALU = mybir.AluOpType
ACT = mybir.ActivationFunctionType

P = 128
D = 256
C = D // P
TPG = 4
GROUP = P * TPG
LAYERS = 3
EPS = 1e-5
FAR = 1 << 20


WIDE = 2 * D


class Memory:
    pass


def wait(engine, sem, count):
    if isinstance(count, int) and count <= 0:
        return
    engine.wait_ge(sem, count)


def run_iterations(engine, n, body):
    body(0)
    if n > 2:
        with engine.Fori(1, n - 1) as i:
            body(i)
    body(n - 1)


def group_of(table, g):
    return table[bass.ds(g * GROUP, GROUP), :].rearrange("(p j) d -> p (j d)", j=TPG)


def last_group_of(m, table):
    return table[(m.NG - 1) * GROUP:m.N, :].rearrange("(p j) d -> p (j d)", j=TPG)


def prepare_constants_and_weights(nc, m):
    EK, EFULL, EREST = m.EK, m.EFULL, m.EREST
    with ExitStack() as ctx:
        def sem(name):
            return ctx.enter_context(nc.semaphore("prep_" + name))

        win_s, w0_s, w_in_s = sem("w_in_in"), sem("layer0_in"), sem("weights_in")
        rows_s, edges_s, first_s = sem("rows_in"), sem("edges_in"), sem("first_constants")
        const_s, dve_s, act_s, pe_s = sem("constants"), sem("dve"), sem("act"), sem("pe")
        parts_s, bo3_s, pads_s = sem("b_out_parts"), sem("b_out_3"), sem("edge_pads")
        bin_s, win_t_s = sem("b_in_spread"), sem("w_in_transposed")
        block = ctx.enter_context(nc.Block())

        @block.sync
        def _(sp):
            def load_layer(l, sem_):
                sp.dma_start(m.w_f[l][:, :, 0:D],
                             m.w_self[l].rearrange("(c p) n -> p c n", p=P)).then_inc(sem_, 16)
                sp.dma_start(m.w_f[l][:, :, D:WIDE],
                             m.w_agg[l].rearrange("(c p) n -> p c n", p=P)).then_inc(sem_, 16)

            sp.dma_start(m.win_f[:, :, :], m.w_in.rearrange("(c p) n -> p c n", p=P)).then_inc(win_s, 16)
            load_layer(0, w0_s)
            sp.dma_start(m.brows[0:1, :], m.b_hid.rearrange("(o l) n -> o (l n)", o=1)).then_inc(rows_s, 16)
            sp.dma_start(m.bo_row[0:1, :], m.b_out.rearrange("(o n) -> o n", o=1)).then_inc(rows_s, 16)
            with nc.allow_non_contiguous_dma(reason="256 numbers"):
                sp.dma_start(m.bin_c[:, :], m.b_in.rearrange("(c p) -> p c", p=P)).then_inc(rows_s, 16)
            sp.wait_ge(pads_s, 2)
            for column, array in ((m.tgt_i, m.src), (m.src_i, m.dst)):
                even = EFULL // 16 * 16
                for a, b in ((0, even), (even, EFULL)):
                    if b > a:
                        sp.dma_start(column[a:b, :],
                                     array[a * EK:b * EK].rearrange("(p k) -> p k", k=EK)).then_inc(edges_s, 16)
                if EREST:
                    sp.dma_start(column[EFULL:EFULL + 1, 0:EREST],
                                 array[EFULL * EK:EFULL * EK + EREST].rearrange("(o k) -> o k", o=1)
                                 ).then_inc(edges_s, 16)
            sp.dma_start(m.in_buf[:, 0, :], group_of(m.x, 0)).then_inc(m.x0_in[0], 16)
            for l in range(1, LAYERS):
                load_layer(l, w_in_s)
            sp.dma_start(m.w_f[LAYERS][:, :, :],
                         m.w_out.rearrange("(c p) n -> p c n", p=P)).then_inc(w_in_s, 16)
            sp.dma_start(m.in_buf[:, 1, :], group_of(m.x, 1)).then_inc(m.x0_in[1], 16)
            sp.wait_ge(parts_s, 1)
            sp.dma_start(m.bo_3[:, :], m.bo_parts[0:1, :, :]).then_inc(bo3_s, 16)
            sp.wait_ge(bo3_s, 16)

        edge_loads = 2 * ((EFULL >= 16) + (EFULL % 16 > 0) + (EREST > 0))

        @block.gpsimd
        def _(pool):
            g = nc.gpsimd
            g.memset(m.tgt_i[:, :], m.NROW).then_inc(pads_s, 1)
            g.memset(m.src_i[:, :], 0).then_inc(pads_s, 1)
            g.memset(m.ident[:, :], 0.0).then_inc(const_s, 1)
            g.memset(m.ones_f[:, :], 1.0).then_inc(const_s, 1)
            pool.wait_ge(const_s, 2)
            g.affine_select(out=m.ident[:, :], in_=m.ident[:, :], compare_op=ALU.not_equal, fill=1.0, base=0,
                            pattern=[[-1, P]], channel_multiplier=1).then_inc(first_s, 1)
            g.affine_select(out=m.after_f[:, :], in_=m.ones_f[:, :], compare_op=ALU.is_gt, fill=0.0, base=0,
                            pattern=[[-1, P]], channel_multiplier=1).then_inc(const_s, 1)
            g.affine_select(out=m.before_f[:, :], in_=m.ones_f[:, :], compare_op=ALU.is_gt, fill=0.0, base=0,
                            pattern=[[1, P]], channel_multiplier=-1).then_inc(const_s, 1)
            g.iota(m.iota_i[:, :], pattern=[[1, max(m.NT, P)]], base=0, channel_multiplier=0).then_inc(const_s, 1)
            g.memset(m.ones_b[:, :], 1.0).then_inc(const_s, 1)
            g.memset(m.zeros_b[:, :], 0.0).then_inc(const_s, 1)
            g.memset(m.eps[:, :], EPS).then_inc(const_s, 1)
            g.memset(m.gath[:, :, :], 0.0).then_inc(const_s, 1)

        @block.scalar
        def _(act):
            act.wait_ge(pe_s, 2)
            nc.scalar.activation(m.w_hi[0][:, :, :], m.ps[:, 1:3, :], ACT.Copy).then_inc(act_s, 1)
            act.wait_ge(w_in_s, 16 * (2 * LAYERS - 1))
            for l in range(1, LAYERS + 1):
                nc.scalar.activation(m.w_hi[l][:, :, :], m.w_f[l][:, :, :], ACT.Copy).then_inc(act_s, 1)

        @block.vector
        def _(dve):
            v = nc.vector
            chain = [0]

            def link(ins):
                chain[0] += 1
                ins.then_inc(dve_s, 1)
                dve.wait_ge(dve_s, chain[0])

            dve.wait_ge(first_s, 1)
            dve.wait_ge(rows_s, 48)
            for c in range(C):
                last = v.tensor_scalar(m.bin_b[:, c, :], m.ones_f[:, :], m.bin_c[:, c:c + 1], None, ALU.mult)
            last.then_inc(bin_s, 1)
            dve.wait_ge(pe_s, 1)
            v.tensor_copy(m.winT[:, :, :].rearrange("p c n -> p (c n)"), m.ps[:, 0, :]).then_inc(win_t_s, 1)
            dve.wait_ge(const_s, 9)
            v.tensor_copy(m.iota_f[:, :], m.iota_i[:, 0:P])
            v.tensor_copy(m.iota_h[:, :], m.iota_i[:, 0:m.NT])
            v.tensor_copy(m.before[:, :], m.before_f[:, :])
            v.tensor_scalar(m.notbefore[:, :], m.before_f[:, :], -1.0, 1.0, ALU.mult, ALU.add)
            link(v.tensor_copy(m.bo_parts[0:1, 0, :], m.bo_row[0:1, :]))
            link(v.tensor_tensor(m.bo_rest[0:1, 0, :], m.bo_row[0:1, :], m.bo_parts[0:1, 0, :], ALU.subtract))
            link(v.tensor_copy(m.bo_parts[0:1, 1, :], m.bo_rest[0:1, 0, :]))
            link(v.tensor_tensor(m.bo_rest[0:1, 1, :], m.bo_rest[0:1, 0, :], m.bo_parts[0:1, 1, :],
                                 ALU.subtract))
            v.tensor_copy(m.bo_parts[0:1, 2, :], m.bo_rest[0:1, 1, :]).then_inc(parts_s, 1)
            dve.wait_ge(edges_s, 16 * edge_loads)
            v.tensor_copy(m.tgt_f[:, :], m.tgt_i[:, :])
            v.tensor_scalar(m.e_tmp[:, :], m.tgt_i[:, :], 9, 2, ALU.logical_shift_right, ALU.logical_shift_left)
            link(v.tensor_scalar(m.e_tmp2[:, :], m.tgt_i[:, :], 3, None, ALU.bitwise_and))
            link(v.tensor_tensor(m.bucket_f[:, :], m.e_tmp[:, :], m.e_tmp2[:, :], ALU.add))
            link(v.tensor_scalar(m.e_tmp[:, :], m.tgt_i[:, :], 2, P - 1, ALU.logical_shift_right, ALU.bitwise_and))
            link(v.tensor_copy(m.lo_f[:, :], m.e_tmp[:, :]))
            link(v.tensor_scalar(m.e_tmp2[:, :], m.src_i[:, :], 4095, None, ALU.bitwise_and))
            link(v.tensor_copy(m.num_lo_f[:, :], m.e_tmp2[:, :]))
            link(v.tensor_tensor(m.e_tmp[:, :], m.src_i[:, :], m.e_tmp2[:, :], ALU.subtract))
            link(v.tensor_scalar(m.num_hi_f[:, :], m.lo_f[:, :], 1.0, 65536.0, ALU.add, ALU.mult))
            link(v.tensor_tensor(m.num_hi_f[:, :], m.num_hi_f[:, :], m.e_tmp[:, :], ALU.add))
            dve.wait_ge(act_s, 1)
            v.tensor_tensor(m.w_lo[0][:, :, :], m.ps[:, 1:3, :], m.w_hi[0][:, :, :].bitcast(F32), ALU.subtract)
            for l in range(1, LAYERS + 1):
                dve.wait_ge(act_s, l + 1)
                v.tensor_tensor(m.w_lo[l][:, :, :], m.w_f[l][:, :, :], m.w_hi[l][:, :, :].bitcast(F32), ALU.subtract)
            dve.wait_ge(pe_s, 3)
            link(v.tensor_copy(m.bias0[:, :], m.ps[:, 3, :]))
            v.tensor_tensor(m.bias0[:, 0:D], m.bias0[:, 0:D], m.ps[:, 4, 0:D], ALU.add)
            for l in (1, 2):
                for t in range(2):
                    v.tensor_copy(m.bias_p[l][:, t, :], m.ps[:, 4 + l // 2, (l % 2) * D:(l % 2) * D + D])

        @block.tensor
        def _(pe):
            t = nc.tensor
            pe.wait_ge(win_s, 16)
            pe.wait_ge(first_s, 1)
            for h in range(C):
                for c in range(C):
                    last = t.transpose(m.ps[:, 0, h * D + c * P:h * D + (c + 1) * P],
                                       m.win_f[:, c, h * P:(h + 1) * P], m.ident[:, :])
            last.then_inc(pe_s, 1)
            pe.wait_ge(win_t_s, 1)
            pe.wait_ge(w0_s, 32)
            for c in range(C):
                for h in range(C):
                    last = t.matmul(m.ps[:, 1 + c, :], m.winT[:, h, c * P:(c + 1) * P], m.w_f[0][:, h, :],
                                    start=h == 0, stop=h == C - 1)
            last.then_inc(pe_s, 1)
            pe.wait_ge(bin_s, 1)
            for h in range(C):
                t.matmul(m.ps[:, 3, :], m.bin_b[:, h, :], m.w_f[0][:, h, :], start=h == 0, stop=h == C - 1)
            pe.wait_ge(rows_s, 48)
            t.matmul(m.ps[:, 4, :], m.ones_f[0:1, :], m.brows[0:1, 0:2 * D], start=True, stop=True)
            t.matmul(m.ps[:, 5, 0:D], m.ones_f[0:1, :], m.brows[0:1, 2 * D:3 * D],
                     start=True, stop=True).then_inc(pe_s, 1)


def load_first_p(m, sp, layer, q):
    sp.dma_start(m.in_buf[:, q, :], group_of(m.p_tab[layer], q)).then_inc(m.p_in[layer][q], 16)


def split_products(nc, m, out_ap, slot, tile, layer, start=True):
    n = 0
    for c in range(C):
        for h, w in ((m.hT_hi, m.w_hi), (m.hT_hi, m.w_lo), (m.hT_lo, m.w_hi)):
            last = nc.tensor.matmul(out_ap, h[:, slot, tile, c, :], w[layer][:, c, :],
                                    start=start and n == 0, stop=n == 3 * C - 1)
            n += 1
    return last


def finish_tables(nc, m, dve, dve_s):
    RANK, DEG, SLOT = 0, 1, 2
    NT = m.NT
    v = nc.vector
    chain = [0]

    def link(ins):
        chain[0] += 1
        ins.then_inc(dve_s, 1)
        dve.wait_ge(dve_s, chain[0])

    link(v.tensor_scalar(m.tab_a[:, :], m.ps[:, DEG, 0:NT], 1.0, None, ALU.max))
    v.reciprocal(m.inv_deg[:, :], m.tab_a[:, :])
    link(v.tensor_scalar(m.full_m[:, :], m.ps[:, RANK, 0:NT], float(P), None, ALU.is_gt))
    link(v.reduce_max(m.flag_f[:, :], m.full_m[:, :], mybir.AxisListType.X))
    link(v.tensor_copy(m.flag_i[:, :], m.flag_f[:, :]))
    link(v.tensor_copy(m.slot_i[:, :], m.ps[:, SLOT, 0:NT]))
    link(v.tensor_scalar(m.slot_src[:, :], m.slot_i[:, :], 16, None, ALU.logical_shift_right))
    link(v.tensor_copy(m.slot_lo[:, :], m.slot_src[:, :]))
    link(v.tensor_scalar(m.tab_b[:, :], m.full_m[:, :], float(-2 * P), -1.0, ALU.mult, ALU.add))
    v.tensor_scalar(m.slot_i[:, :], m.slot_i[:, :], 65535, None, ALU.bitwise_and)
    link(v.tensor_tensor(m.slot_lo[:, :], m.slot_lo[:, :], m.tab_b[:, :], ALU.add))
    v.tensor_copy(m.tab_a[:, :], m.slot_i[:, :])
    link(v.tensor_scalar(m.tab_b[:, :], m.slot_lo[:, :], 0.0, float(FAR), ALU.is_lt, ALU.mult))
    link(v.tensor_tensor(m.slot_src[:, :], m.tab_a[:, :], m.tab_b[:, :], ALU.add))


def first_pass_and_buckets(nc, m):
    NT, NI, EK = m.NT, m.NI, m.EK
    RANK, DEG, SLOT, HT, O = 0, 1, 2, 3, 5
    with ExitStack() as ctx:
        def sem(name):
            return ctx.enter_context(nc.semaphore("p0_" + name))

        x_in = m.x0_in
        stored = [sem(f"stored{q}") for q in range(2)]
        transposed, hi_done, lo_done = sem("transposed"), sem("hi_done"), sem("lo_done")
        multiplied, p_evacuated, t_evacuated = sem("multiplied"), sem("p_evacuated"), sem("t_evacuated")
        t_biased, issue = sem("t_biased"), sem("issue")
        onehot_done, ranked = sem("onehot_done"), sem("ranked")
        rank_read, at_slot_done, counted = sem("rank_read"), sem("at_slot_done"), sem("counted")
        tables = sem("tables")
        block = ctx.enter_context(nc.Block())

        @block.sync
        def _(sp):
            def load(g, q):
                sp.dma_start(m.in_buf[:, q, :], group_of(m.x, g)).then_inc(x_in[q], 16)

            def body(i):
                for q in range(2):
                    g = 2 * i + q
                    wait(sp, transposed, TPG * g + TPG)
                    if isinstance(i, int) and i == NI - 2 and q == 1:
                        sp.dma_start(m.in_buf[0:m.LASTP, q, :], last_group_of(m, m.x)).then_inc(x_in[q], 16)
                    elif isinstance(i, int) and i == NI - 1:
                        wait(sp, stored[q], 32)
                        load_first_p(m, sp, 0, q)
                    else:
                        load(g + 2, q)
                    wait(sp, p_evacuated, TPG * g + TPG)
                    sp.dma_start(group_of(m.p_tab[0], g), m.p_out[:, q, :]).then_inc(stored[q], 16)
                    wait(sp, t_biased, TPG * g + TPG)
                    sp.dma_start(group_of(m.t_tab[0], g), m.t_out[:, q, :]).then_inc(stored[q], 16)

            body(0)
            if NI > 3:
                with sp.Fori(1, NI - 2) as i:
                    body(i)
            body(NI - 2)
            body(NI - 1)
            for q in range(2):
                sp.wait_ge(stored[q], 32 * NI)

        @block.scalar
        def _(act):
            def split_hi(t, r):
                wait(act, transposed, t + 1)
                wait(act, multiplied, t - 3)
                nc.scalar.activation(m.hT_hi[:, (r // 2) % 2, r % 2, :, :],
                                     m.ps[:, HT + r % 2, 0:D], ACT.Copy).then_inc(hi_done, 1)

            def evacuate_t(t, j):
                wait(act, multiplied, t + 1)
                wait(act, t_biased, t - 3)
                nc.scalar.activation(m.t_raw[:, j % 4, :], m.ps[:, O + j % 2, D:WIDE],
                                     ACT.Copy).then_inc(t_evacuated, 1)

            def body(i):
                for j in range(8):
                    if not (isinstance(i, int) and i == NI - 1 and j == 7):
                        split_hi(8 * i + j + 1, j + 1)
                    evacuate_t(8 * i + j, j)

            split_hi(0, 0)
            run_iterations(act, NI, body)

        @block.gpsimd
        def _(pool):
            def body(i):
                for j in range(8):
                    q = j // TPG
                    c = (j % TPG) * D
                    if j % TPG == 0 and not (isinstance(i, int) and i == 0):
                        wait(pool, stored[q], 32 * i)
                        pool.sem_inc(issue, 1)
                    wait(pool, t_evacuated, 8 * i + j + 1)
                    nc.gpsimd.tensor_tensor(m.t_out[:, q, c:c + D], m.t_raw[:, j % 4, :], m.bias0[:, D:WIDE],
                                            ALU.add).then_inc(t_biased, 1)

            run_iterations(pool, NI, body)

        @block.vector
        def _(dve):
            v = nc.vector

            def split_lo(t, r):
                wait(dve, hi_done, t + 1)
                wait(dve, multiplied, t - 3)
                hi = m.hT_hi[:, (r // 2) % 2, r % 2, :, :].rearrange("p c n -> p (c n)").bitcast(F32)
                v.tensor_tensor(m.hT_lo[:, (r // 2) % 2, r % 2, :, :].rearrange("p c n -> p (c n)"),
                                m.ps[:, HT + r % 2, 0:D], hi, ALU.subtract).then_inc(lo_done, 1)

            def onehots(k, q):
                wait(dve, counted, k - 1)
                v.tensor_scalar(m.oh_bucket[:, q, :], m.iota_h[:, :], m.bucket_f[:, bass.ds(k, 1)], None,
                                ALU.is_equal)
                v.tensor_scalar(m.oh_lo[:, q, :], m.iota_f[:, :], m.lo_f[:, bass.ds(k, 1)], None,
                                ALU.is_equal).then_inc(onehot_done, 1)

            def slots(k, q):
                wait(dve, ranked, k + 1)
                v.tensor_tensor_reduce(out=m.junk[:, :], in0=m.ps[:, RANK, 0:NT], in1=m.oh_bucket[:, q, :].bitcast(F32),
                                       scale=1.0, scalar=0.0, op0=ALU.mult, op1=ALU.add,
                                       accum_out=m.rank[:, q:q + 1]).then_inc(rank_read, 1)
                wait(dve, rank_read, k + 1)
                for n, number in enumerate((m.num_lo_f, m.num_hi_f)):
                    last = v.tensor_scalar(m.at_slot[:, q, n, :], m.iota_f[:, :], m.rank[:, q:q + 1],
                                           number[:, bass.ds(k, 1)], ALU.is_equal, ALU.mult)
                last.then_inc(at_slot_done, 1)

            def evacuate_p(t, i, j):
                q = j // TPG
                wait(dve, t_evacuated, t + 1)
                if j % TPG == 0:
                    wait(dve, stored[q], 32 * i)
                c = (j % TPG) * D
                v.tensor_tensor(m.p_out[:, q, c:c + D], m.ps[:, O + j % 2, 0:D], m.bias0[:, 0:D],
                                ALU.add).then_inc(p_evacuated, 1)

            def body(i):
                final = isinstance(i, int) and i == NI - 1
                for j in range(8):
                    t = 8 * i + j
                    k = 4 * i + j // 2
                    if not (final and j == 7):
                        split_lo(t + 1, j + 1)
                    if j % 2 == 0:
                        slots(k, (j // 2) % 2)
                    elif not (final and j == 7):
                        onehots(k + 1, (j // 2 + 1) % 2)
                    evacuate_p(t, i, j)

            onehots(0, 0)
            split_lo(0, 0)
            run_iterations(dve, NI, body)
            dve.wait_ge(counted, EK)
            finish_tables(nc, m, dve, tables)

        @block.tensor
        def _(pe):
            def transposes(t, i, r):
                if r % TPG == 0:
                    wait(pe, x_in[(r // TPG) % 2], 16 * i + 16)
                wait(pe, hi_done, t - 1)
                wait(pe, lo_done, t - 1)
                src = m.in_buf[:, (r // TPG) % 2, (r % TPG) * D:(r % TPG) * D + D]
                for c in range(C):
                    last = nc.tensor.transpose(m.ps[:, HT + r % 2, c * P:(c + 1) * P],
                                               src[:, c * P:(c + 1) * P], m.ident[:, :])
                last.then_inc(transposed, 1)

            def counts(bank, lhs, q):
                return nc.tensor.matmul(m.ps[:, bank, 0:NT], lhs, m.oh_bucket[:, q, :], start=False, stop=True,
                                        skip_group_check=True)

            def body(i):
                final = isinstance(i, int) and i == NI - 1
                for j in range(8):
                    t = 8 * i + j
                    k = 4 * i + j // 2
                    q = (j // 2) % 2
                    if not (final and j == 7):
                        transposes(t + 1, i + (j + 1) // 8, (j + 1) % 8)
                    if j % 2 == 0:
                        wait(pe, onehot_done, k + 1)
                        counts(RANK, m.before[:, :], q).then_inc(ranked, 1)
                    wait(pe, hi_done, t + 1)
                    wait(pe, lo_done, t + 1)
                    wait(pe, p_evacuated, t - 1)
                    split_products(nc, m, m.ps[:, O + j % 2, :], (j // 2) % 2, j % 2, 0).then_inc(multiplied, 1)
                    if j % 2 == 1:
                        wait(pe, at_slot_done, k + 1)
                        counts(RANK, m.notbefore[:, :], q)
                        counts(DEG, m.oh_lo[:, q, :], q)
                        for n in range(2):
                            last = counts(SLOT, m.at_slot[:, q, n, :], q)
                        last.then_inc(counted, 1)

            for bank in (RANK, DEG, SLOT):
                nc.tensor.matmul(m.ps[:, bank, 0:NT], m.zeros_b[:, 0:P], m.zeros_b[:, 0:NT], start=True, stop=True,
                                 skip_group_check=True)
            transposes(0, 0, 0)
            run_iterations(pe, NI, body)


def add_overfull_buckets(nc, m, layer):
    EK, NT, NROW = m.EK, m.NT, m.NROW
    TARGETS, SUMS, LO_T, WEIGHTS = 0, 1, 2, 3
    NEW, OLD = 0, 1
    STEPS = 8
    with ExitStack() as ctx:
        def sem(name):
            return ctx.enter_context(nc.semaphore(f"over{layer}_{name}"))

        turn, issue = sem("turn"), sem("issue")
        spread_done, targets_done, same_done = sem("spread_done"), sem("targets_done"), sem("same_done")
        weights_done, index_done = sem("weights_done"), sem("index_done")
        rows_in, old_in, written = sem("rows_in"), sem("old_in"), sem("written")
        reloaded = sem("reloaded")
        summed, added, dve_s = sem("summed"), sem("added"), sem("dve")
        block = ctx.enter_context(nc.Block())

        def if_overfull(engine):
            flag = engine.value_load(m.flag_i[0:1, 0:1], min_val=0, max_val=1)
            return engine.If(flag)

        @block.sync
        def _(sp):
            for q in range(2):
                sp.wait_ge(m.p_in[layer][q], 16)
            with if_overfull(sp):
                sp.wait_ge(written, 16 * EK)
                for q in range(2):
                    sp.dma_start(m.in_buf[:, q, :], group_of(m.p_tab[layer], q)).then_inc(reloaded, 16)
                sp.wait_ge(reloaded, 32)

        @block.gpsimd
        def _(pool):
            def indexed(out, out_offset, in_, in_offset, sem_):
                nc.gpsimd.indirect_dma_start(out=out, out_offset=out_offset, in_=in_, in_offset=in_offset,
                                             bounds_check=NROW - 1, oob_is_err=False).then_inc(sem_, 16)

            with if_overfull(pool):
                pool.sem_inc(turn, 1)
                with pool.Fori(0, EK) as k:
                    pool.wait_ge(spread_done, k + 1)
                    pool.sem_inc(issue, 1)
                    indexed(m.gath[:, NEW, :], None, m.t_tab[layer][:, :],
                            bass.IndirectOffsetOnAxis(ap=m.over_src[:, :], axis=0), rows_in)
                    pool.wait_ge(index_done, k + 1)
                    pool.sem_inc(issue, 1)
                    indexed(m.gath[:, OLD, :], None, m.p_tab[layer][:, :],
                            bass.IndirectOffsetOnAxis(ap=m.over_row[:, :], axis=0), old_in)
                    pool.wait_ge(added, k + 1)
                    pool.sem_inc(issue, 1)
                    indexed(m.p_tab[layer][:, :], bass.IndirectOffsetOnAxis(ap=m.over_row[:, :], axis=0),
                            m.v_buf[:, 0, 0, :], None, written)
                    pool.wait_ge(written, 16 * k + 16)
                    pool.sem_inc(turn, 1)

        @block.vector
        def _(dve):
            v = nc.vector
            with if_overfull(dve):
                with dve.Fori(0, EK) as k:
                    n = [0]

                    def link(ins):
                        n[0] += 1
                        ins.then_inc(dve_s, 1)
                        dve.wait_ge(dve_s, STEPS * k + n[0])

                    column = bass.ds(k, 1)
                    dve.wait_ge(turn, k + 1)
                    v.tensor_copy(m.over_src[:, :], m.src_i[:, column])
                    v.tensor_scalar(m.over_bucket[:, :], m.iota_h[:, :], m.bucket_f[:, column], None, ALU.is_equal)
                    v.tensor_scalar(m.over_lo[:, :], m.iota_f[:, :], m.lo_f[:, column], None, ALU.is_equal)
                    v.tensor_scalar(m.over_spread[:, :], m.ones_f[:, :], m.tgt_f[:, column], None,
                                    ALU.mult).then_inc(spread_done, 1)
                    dve.wait_ge(targets_done, k + 1)
                    v.tensor_copy(m.over_loT[:, :], m.ps[:, LO_T, 0:P])
                    v.tensor_scalar(m.over_same[:, :], m.ps[:, TARGETS, 0:P], m.tgt_f[:, column], None,
                                    ALU.is_equal).then_inc(same_done, 1)
                    dve.wait_ge(same_done, k + 1)
                    link(v.tensor_tensor_reduce(out=m.over_earlier[:, :], in0=m.over_same[:, :],
                                                in1=m.after_f[:, :], scale=1.0, scalar=0.0, op0=ALU.mult,
                                                op1=ALU.add, accum_out=m.over_n[:, 0:1]))
                    link(v.tensor_tensor_reduce(out=m.junk[:, :], in0=m.over_bucket[:, :], in1=m.full_m[:, :],
                                                scale=1.0, scalar=0.0, op0=ALU.mult, op1=ALU.add,
                                                accum_out=m.over_n[:, 1:2]))
                    link(v.tensor_scalar(m.over_n[:, 2:3], m.over_n[:, 0:1], 0.0, float(FAR), ALU.is_gt, ALU.mult))
                    link(v.tensor_scalar(m.over_n[:, 3:4], m.over_n[:, 1:2], float(-FAR), float(FAR), ALU.mult,
                                         ALU.add))
                    link(v.tensor_tensor(m.over_n[:, 2:3], m.over_n[:, 2:3], m.over_n[:, 3:4], ALU.add))
                    link(v.tensor_tensor(m.over_n[:, 2:3], m.over_n[:, 2:3], m.tgt_f[:, column], ALU.add))
                    v.tensor_copy(m.over_row[:, :], m.over_n[:, 2:3]).then_inc(index_done, 1)
                    dve.wait_ge(weights_done, k + 1)
                    link(v.tensor_tensor_reduce(out=m.junk[:, :], in0=m.ps[:, WEIGHTS, 0:NT],
                                                in1=m.over_bucket[:, :], scale=1.0, scalar=0.0, op0=ALU.mult,
                                                op1=ALU.add, accum_out=m.over_n[:, 4:5]))
                    dve.wait_ge(summed, k + 1)
                    dve.wait_ge(old_in, 16 * k + 16)
                    link(v.tensor_scalar(m.v_buf[:, 0, 1, :], m.ps[:, SUMS, 0:D], m.over_n[:, 4:5], None, ALU.mult))
                    v.tensor_tensor(m.v_buf[:, 0, 0, :], m.v_buf[:, 0, 1, :], m.gath[:, OLD, :],
                                    ALU.add).then_inc(added, 1)
                    assert n[0] == STEPS

        @block.tensor
        def _(pe):
            with if_overfull(pe):
                with pe.Fori(0, EK) as k:
                    pe.wait_ge(spread_done, k + 1)
                    nc.tensor.matmul(m.ps[:, TARGETS, 0:P], m.over_spread[:, :], m.ident[:, :],
                                     start=True, stop=True)
                    nc.tensor.transpose(m.ps[:, LO_T, 0:P], m.over_lo[:, :], m.ident[:, :]).then_inc(targets_done, 1)
                    pe.wait_ge(same_done, k + 1)
                    nc.tensor.matmul(m.ps[:, WEIGHTS, 0:NT], m.over_loT[:, :], m.inv_deg[:, :],
                                     start=True, stop=True).then_inc(weights_done, 1)
                    pe.wait_ge(rows_in, 16 * k + 16)
                    nc.tensor.matmul(m.ps[:, SUMS, 0:D], m.over_same[:, :], m.gath[:, NEW, :],
                                     start=True, stop=True).then_inc(summed, 1)


class GatheringPass:

    def __init__(self, nc, m, layer, sem):
        self.nc, self.m, self.layer = nc, m, layer
        self.p_in = m.p_in[layer - 1]
        self.gathered = [sem(f"gathered{r}") for r in range(8)]
        self.index_done = sem("index_done")
        self.issue = sem("issue")
        if layer < LAYERS:
            self.gath_hi_done, self.gath_lo_done = sem("gath_hi_done"), sem("gath_lo_done")
        else:
            self.picked_odd = sem("picked_odd")
        self.picked = sem("picked")
        self.summed, self.v_done = sem("summed"), sem("v_done")
        self.transposed, self.hi_done, self.lo_done = sem("transposed"), sem("hi_done"), sem("lo_done")
        self.multiplied = sem("multiplied")

    def at(self, i, j, ahead):
        u = 4 * i + j + ahead
        if isinstance(u, int) and not 0 <= u < 4 * self.m.NI:
            return None
        return u, i + (j + ahead) // 4, (j + ahead) % 4

    def run(self, engine, step, flush=0):
        NI = self.m.NI
        for j in range(1, 4):
            step(-1, j)

        def body(i):
            for j in range(4):
                step(i, j)

        run_iterations(engine, NI, body)
        for j in range(flush):
            step(NI, j)

    def gather_program(self, pool, used, pick_here=False):
        m, nc = self.m, self.nc

        def body(i):
            for h in range(2):
                if not (isinstance(i, int) and i == 0):
                    wait(pool, used, 4 * i + 2 * h - 2)
                    pool.sem_inc(self.issue, 1)
                nc.gpsimd.tensor_copy(m.idx8[:, h, 0:4],
                                      m.slot_src[:, bass.ds(8 * i + 4 * h, 4)]).then_inc(self.index_done, 1)
                if pick_here:
                    nc.gpsimd.tensor_copy(m.lo8[:, h, 0:4],
                                          m.slot_lo[:, bass.ds(8 * i + 4 * h, 4)]).then_inc(self.index_done, 1)
                wait(pool, self.index_done, (2 * i + h + 1) * (1 + pick_here))
                pool.sem_inc(self.issue, 1)
                for n in range(4):
                    nc.gpsimd.indirect_dma_start(
                        out=m.gath[:, 4 * h + n, :], out_offset=None, in_=m.t_tab[self.layer - 1][:, :],
                        in_offset=bass.IndirectOffsetOnAxis(ap=m.idx8[:, h, n:n + 1], axis=0),
                        bounds_check=m.NROW - 1, oob_is_err=False).then_inc(self.gathered[4 * h + n], 16)
                if pick_here:
                    for n in (0, 2):
                        nc.gpsimd.tensor_scalar(m.pick_f[:, 4 * h + n, :], m.iota_f[:, :], m.lo8[:, h, n:n + 1],
                                                None, ALU.is_equal).then_inc(self.picked, 1)

        run_iterations(pool, m.NI, body)

    def split_hi(self, act, i, j):
        m = self.m
        if place := self.at(i, j, 1):
            u, _, r = place
            wait(act, self.transposed, u + 1)
            wait(act, self.multiplied, u - 1)
            self.nc.scalar.activation(m.hT_hi[:, r % 2, :, :, :].rearrange("p t c n -> p (t c n)"),
                                      m.ps[:, 2 + r % 2, :], ACT.Relu).then_inc(self.hi_done, 1)

    def split_gathered_hi(self, act, i, j):
        m = self.m
        if place := self.at(i, j, 3):
            u, n, r = place
            for q in (2 * r, 2 * r + 1):
                wait(act, self.gathered[q], 16 * n + 16)
            wait(act, self.summed, u - 1)
            wait(act, self.gath_lo_done, u - 1)
            self.nc.scalar.activation(m.gath_hi[:, r % 2, :, :], m.gath[:, 2 * r:2 * r + 2, :],
                                      ACT.Copy).then_inc(self.gath_hi_done, 1)

    def split_lo(self, dve, i, j):
        m = self.m
        if place := self.at(i, j, 1):
            u, _, r = place
            wait(dve, self.hi_done, u + 1)
            self.nc.vector.scalar_tensor_tensor(
                out=m.hT_lo[:, r % 2, :, :, :].rearrange("p t c n -> p (t c n)"), in0=m.ps[:, 2 + r % 2, :],
                scalar=0.0, in1=m.hT_hi[:, r % 2, :, :, :].rearrange("p t c n -> p (t c n)").bitcast(F32),
                op0=ALU.max, op1=ALU.subtract).then_inc(self.lo_done, 1)

    def make_v(self, dve, i, j, between=lambda: None):
        m = self.m
        if place := self.at(i, j, 2):
            u, n, r = place
            if r % 2 == 0:
                wait(dve, self.p_in[r // 2], 16 * n + 16)
            wait(dve, self.summed, u + 1)
            wait(dve, self.transposed, u - 1)
            for t in range(2):
                c = (2 * (r % 2) + t) * D
                last = self.nc.vector.scalar_tensor_tensor(
                    out=m.v_buf[:, r % 2, t, :], in0=m.ps[:, r % 2, t * D:(t + 1) * D],
                    scalar=m.inv_deg[:, bass.ds(2 * u + t, 1)], in1=m.in_buf[:, r // 2, c:c + D],
                    op0=ALU.mult, op1=ALU.add)
                if t == 0:
                    between()
            last.then_inc(self.v_done, 1)
        else:
            between()

    def split_gathered_lo(self, dve, i, j):
        m = self.m
        if place := self.at(i, j, 3):
            u, _, r = place
            wait(dve, self.gath_hi_done, u + 1)
            self.nc.vector.tensor_tensor(m.gath_lo[:, r % 2, :, :], m.gath[:, 2 * r:2 * r + 2, :],
                                         m.gath_hi[:, r % 2, :, :].bitcast(F32),
                                         ALU.subtract).then_inc(self.gath_lo_done, 1)

    def make_pick(self, dve, i, j):
        m = self.m
        if place := self.at(i, j, 3):
            u, _, r = place
            wait(dve, self.summed, u - 1)
            for t in range(2):
                last = self.nc.vector.tensor_scalar(m.pick[:, r % 2, t, :], m.iota_f[:, :],
                                                    m.slot_lo[:, bass.ds(2 * u + t, 1)], None, ALU.is_equal)
            last.then_inc(self.picked, 1)

    def make_pick_odd(self, dve, i, j):
        m = self.m
        if place := self.at(i, j, 3):
            u, _, r = place
            wait(dve, self.summed, u - 3)
            self.nc.vector.tensor_scalar(m.pick_f[:, 2 * r + 1, :], m.iota_f[:, :],
                                         m.slot_lo[:, bass.ds(2 * u + 1, 1)], None,
                                         ALU.is_equal).then_inc(self.picked_odd, 1)

    def sum_per_node(self, pe, i, j):
        m = self.m
        if place := self.at(i, j, 2):
            u, _, r = place
            wait(pe, self.gath_lo_done, u + 1)
            wait(pe, self.picked, u + 1)
            wait(pe, self.v_done, u - 1)
            for t in range(2):
                for n, rows in enumerate((m.gath_hi, m.gath_lo)):
                    last = self.nc.tensor.matmul(m.ps[:, r % 2, t * D:(t + 1) * D], m.pick[:, r % 2, t, :],
                                                 rows[:, r % 2, t, :], start=n == 0, stop=n == 1)
            last.then_inc(self.summed, 1)

    def sum_per_node_unsplit(self, pe, i, j):
        m = self.m
        if place := self.at(i, j, 2):
            u, n, r = place
            for q in (2 * r, 2 * r + 1):
                wait(pe, self.gathered[q], 16 * n + 16)
            wait(pe, self.picked, u + 1)
            wait(pe, self.picked_odd, u + 1)
            wait(pe, self.v_done, u - 1)
            for t in range(2):
                last = self.nc.tensor.matmul(m.ps[:, r % 2, t * D:(t + 1) * D], m.pick_f[:, 2 * r + t, :],
                                             m.gath[:, 2 * r + t, :], start=True, stop=True)
            last.then_inc(self.summed, 1)

    def transpose_v(self, pe, i, j):
        m = self.m
        if place := self.at(i, j, 1):
            u, _, r = place
            wait(pe, self.v_done, u + 1)
            wait(pe, self.lo_done, u - 1)
            for t in range(2):
                for c in range(C):
                    last = self.nc.tensor.transpose(m.ps[:, 2 + r % 2, (2 * t + c) * P:(2 * t + c + 1) * P],
                                                    m.v_buf[:, r % 2, t, c * P:(c + 1) * P], m.ident[:, :])
            last.then_inc(self.transposed, 1)


def middle_pass(nc, m, layer):
    NI = m.NI
    with ExitStack() as ctx:
        def sem(name):
            return ctx.enter_context(nc.semaphore(f"p{layer}_{name}"))

        g = GatheringPass(nc, m, layer, sem)
        stored = [sem(f"stored{q}") for q in range(2)]
        p_evacuated, t_evacuated = sem("p_evacuated"), sem("t_evacuated")
        block = ctx.enter_context(nc.Block())

        @block.sync
        def _(sp):
            def load(group, q):
                sp.dma_start(m.in_buf[:, q, :], group_of(m.p_tab[layer - 1], group)).then_inc(g.p_in[q], 16)

            def body(i):
                for q in range(2):
                    group = 2 * i + q
                    wait(sp, g.v_done, 2 * group + 2)
                    if isinstance(i, int) and i == NI - 1:
                        wait(sp, stored[q], 32)
                        load_first_p(m, sp, layer, q)
                    else:
                        load(group + 2, q)
                    wait(sp, t_evacuated, 2 * group + 2)
                    sp.dma_start(group_of(m.t_tab[layer], group), m.t_out[:, q, :]).then_inc(stored[q], 16)
                    wait(sp, p_evacuated, 2 * group + 2)
                    sp.dma_start(group_of(m.p_tab[layer], group), m.p_out[:, q, :]).then_inc(stored[q], 16)

            run_iterations(sp, NI, body)
            for q in range(2):
                sp.wait_ge(stored[q], 32 * NI)

        @block.gpsimd
        def _(pool):
            g.gather_program(pool, g.gath_lo_done)

        @block.scalar
        def _(act):
            def evacuate_t(i, j):
                if place := g.at(i, j, 0):
                    u, n, r = place
                    wait(act, g.multiplied, u + 1)
                    if r % 2 == 0:
                        wait(act, stored[r // 2], 32 * n)
                    nc.scalar.activation(
                        m.t_out[:, r // 2, (r % 2) * WIDE:(r % 2 + 1) * WIDE].rearrange("p (t d) -> p t d", t=2),
                        m.ps[:, 4 + 2 * (r % 2):6 + 2 * (r % 2), D:WIDE], ACT.Copy).then_inc(t_evacuated, 1)

            def step(i, j):
                g.split_gathered_hi(act, i, j)
                g.split_hi(act, i, j)
                evacuate_t(i, j)

            g.run(act, step)

        @block.vector
        def _(dve):
            def evacuate_p(i, j):
                if place := g.at(i, j, 0):
                    u, n, r = place
                    wait(dve, t_evacuated, u + 1)
                    if r % 2 == 0:
                        wait(dve, stored[r // 2], 32 * n)
                    nc.vector.tensor_tensor(
                        m.p_out[:, r // 2, (r % 2) * WIDE:(r % 2 + 1) * WIDE].rearrange("p (t d) -> p t d", t=2),
                        m.ps[:, 4 + 2 * (r % 2):6 + 2 * (r % 2), 0:D], m.bias_p[layer][:, :, :],
                        ALU.add).then_inc(p_evacuated, 1)

            def step(i, j):
                g.split_gathered_lo(dve, i, j)
                g.make_pick(dve, i, j)
                g.make_v(dve, i, j)
                g.split_lo(dve, i, j)
                evacuate_p(i, j)

            g.run(dve, step)

        @block.tensor
        def _(pe):
            def multiply(i, j):
                if place := g.at(i, j, 0):
                    u, _, r = place
                    wait(pe, g.lo_done, u + 1)
                    wait(pe, p_evacuated, u - 1)
                    for t in range(2):
                        last = split_products(nc, m, m.ps[:, 4 + 2 * (r % 2) + t, :], r % 2, t, layer)
                    last.then_inc(g.multiplied, 1)

            def step(i, j):
                g.sum_per_node(pe, i, j)
                g.transpose_v(pe, i, j)
                multiply(i, j)

            g.run(pe, step)


def last_pass(nc, m):
    NI = m.NI
    with ExitStack() as ctx:
        def sem(name):
            return ctx.enter_context(nc.semaphore(f"p{LAYERS}_{name}"))

        g = GatheringPass(nc, m, LAYERS, sem)
        x_in = [sem(f"x_in{q}") for q in range(2)]
        stored = [sem(f"stored{q}") for q in range(2)]
        y_done, mean_done, squared = sem("y_done"), sem("mean_done"), sem("squared")
        root_done, scale_done = sem("root_done"), sem("scale_done")
        normed, dve_s = sem("normed"), sem("dve")
        block = ctx.enter_context(nc.Block())

        @block.sync
        def _(sp):
            def load_p(group, q):
                sp.dma_start(m.in_buf[:, q, :], group_of(m.p_tab[LAYERS - 1], group)).then_inc(g.p_in[q], 16)

            def load_x(group, q, last):
                if last:
                    sp.dma_start(m.x_buf[0:m.LASTP, q, :], last_group_of(m, m.x)).then_inc(x_in[q], 16)
                else:
                    sp.dma_start(m.x_buf[:, q, :], group_of(m.x, group)).then_inc(x_in[q], 16)

            def store(group, q, last=False):
                wait(sp, normed, 2 * group + 2)
                if last:
                    sp.dma_start(last_group_of(m, m.out), m.p_out[0:m.LASTP, q, :]).then_inc(stored[q], 16)
                else:
                    sp.dma_start(group_of(m.out, group), m.p_out[:, q, :]).then_inc(stored[q], 16)

            def body(i):
                from_end = m.NI - i if isinstance(i, int) else None
                for q in range(2):
                    group = 2 * i + q
                    if from_end != 1:
                        wait(sp, y_done, 2 * group + 2)
                        load_x(group + 2, q, from_end == 2 and q == 1)
                        if not (from_end == 2 and q == 1):
                            wait(sp, g.v_done, 2 * group + 4)
                            load_p(group + 3, 1 - q)
                    if not (isinstance(group, int) and group == 0):
                        store(group - 1, 1 - q)

            for q in range(2):
                load_x(q, q, False)
            wait(sp, g.v_done, 2)
            load_p(2, 0)
            body(0)
            if NI > 3:
                with sp.Fori(1, NI - 2) as i:
                    body(i)
            body(NI - 2)
            body(NI - 1)
            store(m.NG - 1, 1, last=True)
            for q in range(2):
                sp.wait_ge(stored[q], 16 * NI)

        @block.gpsimd
        def _(pool):
            g.gather_program(pool, g.summed, pick_here=True)

        @block.scalar
        def _(act):
            def mean_and_root(i, j):
                if place := g.at(i, j, -1):
                    u, _, r = place
                    wait(act, y_done, u + 1)
                    nc.scalar.activation(m.minus_mean[:, 2 * r:2 * r + 2], m.y_sum[:, 2 * r:2 * r + 2], ACT.Copy,
                                         scale=-1.0 / D).then_inc(mean_done, 1)
                    wait(act, mean_done, u + 1)
                    for k in (2 * r, 2 * r + 1):
                        last = nc.scalar.activation(m.square[:, k, :], m.y_buf[:, k, :], ACT.Square,
                                                    bias=m.minus_mean[:, k:k + 1], accum_out=m.squares[:, k:k + 1])
                    last.then_inc(squared, 1)
                    wait(act, squared, u + 1)
                    nc.scalar.activation(m.root[:, 2 * r:2 * r + 2], m.squares[:, 2 * r:2 * r + 2], ACT.Sqrt,
                                         bias=m.eps[:, :], scale=1.0 / D).then_inc(root_done, 1)

            def normalise(i, j):
                if place := g.at(i, j, -3):
                    u, n, r = place
                    wait(act, scale_done, 2 * n + r // 2 + 1)
                    if r % 2 == 0:
                        wait(act, stored[r // 2], 16 * n)
                    for t in range(2):
                        k = 2 * r + t
                        c = (2 * (r % 2) + t) * D
                        last = nc.scalar.activation(m.p_out[:, r // 2, c:c + D], m.y_buf[:, k, :], ACT.Identity,
                                                    bias=m.shift[:, k:k + 1], scale=m.rstd[:, k:k + 1])
                    last.then_inc(normed, 1)

            def step(i, j):
                g.split_hi(act, i, j)
                mean_and_root(i, j)
                normalise(i, j)

            g.run(act, step, flush=3)

        @block.vector
        def _(dve):
            v = nc.vector

            def residual(i, j):
                if place := g.at(i, j, 0):
                    u, n, r = place
                    wait(dve, g.multiplied, u + 1)
                    if r % 2 == 0:
                        wait(dve, x_in[r // 2], 16 * n + 16)
                    wait(dve, normed, u - 3)
                    for t in range(2):
                        k = 2 * r + t
                        c = (2 * (r % 2) + t) * D
                        last = v.scalar_tensor_tensor(
                            out=m.y_buf[:, k, :], in0=m.ps[:, 4 + r % 2, t * D:(t + 1) * D], scalar=1.0,
                            in1=m.x_buf[:, r // 2, c:c + D], op0=ALU.mult, op1=ALU.add,
                            accum_out=m.y_sum[:, k:k + 1])
                    last.then_inc(y_done, 1)

            def scales(i, j):
                place = g.at(i, j, -3)
                if place is None or place[2] % 2:
                    return [lambda: None] * 6
                u, n, r = place
                group = 2 * n + r // 2
                k = slice(2 * r, 2 * r + 4)
                rstd, newton = m.rstd[:, k], m.newton[:, k]

                def invert():
                    wait(dve, root_done, u + 2)
                    v.tensor_scalar(m.ve[:, k], m.squares[:, k], 1.0 / D, EPS, ALU.mult, ALU.add)
                    v.reciprocal(rstd, m.root[:, k]).then_inc(dve_s, 1)

                def times_ve():
                    wait(dve, dve_s, 5 * group + 1)
                    v.tensor_tensor(newton, rstd, m.ve[:, k], ALU.mult).then_inc(dve_s, 1)

                def times_rstd():
                    wait(dve, dve_s, 5 * group + 2)
                    v.tensor_tensor(newton, newton, rstd, ALU.mult).then_inc(dve_s, 1)

                def factor():
                    wait(dve, dve_s, 5 * group + 3)
                    v.tensor_scalar(newton, newton, -0.5, 1.5, ALU.mult, ALU.add).then_inc(dve_s, 1)

                def improve():
                    wait(dve, dve_s, 5 * group + 4)
                    v.tensor_tensor(rstd, rstd, newton, ALU.mult).then_inc(dve_s, 1)

                def shift():
                    wait(dve, dve_s, 5 * group + 5)
                    v.tensor_tensor(m.shift[:, k], m.minus_mean[:, k], rstd, ALU.mult).then_inc(scale_done, 1)

                return invert, times_ve, times_rstd, factor, improve, shift

            def step(i, j):
                invert, times_ve, times_rstd, factor, improve, shift = scales(i, j)
                invert()
                g.make_pick_odd(dve, i, j)
                times_ve()
                g.make_v(dve, i, j, between=times_rstd)
                factor()
                improve()
                g.split_lo(dve, i, j)
                shift()
                residual(i, j)

            g.run(dve, step, flush=3)

        @block.tensor
        def _(pe):
            def multiply(i, j):
                if place := g.at(i, j, 0):
                    u, _, r = place
                    wait(pe, g.lo_done, u + 1)
                    wait(pe, y_done, u - 1)
                    for t in range(2):
                        o = m.ps[:, 4 + r % 2, t * D:(t + 1) * D]
                        nc.tensor.matmul(o, m.ones_b[0:3, :], m.bo_3[0:3, :], start=True, stop=False)
                        last = split_products(nc, m, o, r % 2, t, LAYERS, start=False)
                    last.then_inc(g.multiplied, 1)

            def step(i, j):
                g.sum_per_node_unsplit(pe, i, j)
                g.transpose_v(pe, i, j)
                multiply(i, j)

            g.run(pe, step)


def build_program(nc, x, src, dst, w_in, b_in, w_agg, w_self, b_hid, w_out, b_out, out):
    m = Memory()
    N = x.shape[0]
    E = src.shape[0]
    NG = -(-N // GROUP)
    NT = NG * TPG
    NROW = NG * GROUP
    LASTP = (N - (NG - 1) * GROUP) // TPG
    EK = 2 * NG
    EFULL = E // EK
    EREST = E - EFULL * EK
    NI = NG // 2
    assert NG % 2 == 0 and NG >= 6 and E <= EK * P and NT <= 512 and NROW <= 65536
    assert N % TPG == 0 and NROW < FAR

    with ExitStack() as ctx:
        def sb(name, shape, dt):
            return ctx.enter_context(nc.sbuf_tensor(name, shape, dt))

        m.p_tab = [nc.dram_tensor(f"p_tab{l}", [NROW, D], F32, kind="Internal").ap() for l in range(LAYERS)]
        m.t_tab = [nc.dram_tensor(f"t_tab{l}", [NROW, D], F32, kind="Internal").ap() for l in range(LAYERS)]

        m.ident = sb("ident", [P, P], F32)
        m.iota_i = sb("iota_i", [P, max(NT, P)], I32)
        m.iota_f = sb("iota_f", [P, P], F32)
        m.iota_h = sb("iota_h", [P, NT], F16)
        m.before = sb("before", [P, P], F32R)
        m.notbefore = sb("notbefore", [P, P], F32R)
        m.after_f = sb("after_f", [P, P], F32)
        m.zeros_b = sb("zeros_b", [P, 512], BF16)
        m.ones_f = sb("ones_f", [P, P], F32)
        m.before_f = sb("before_f", [P, P], F32)
        m.ones_b = sb("ones_b", [3, P], BF16)

        m.w_f = [sb(f"w_f{l}", [P, C, WIDE], F32) for l in range(LAYERS)]
        m.w_f.append(sb("wo_f", [P, C, D], F32))
        m.win_f = sb("win_f", [P, C, D], F32)
        m.winT = sb("winT", [P, C, D], F32)
        widths = [WIDE] * LAYERS + [D]
        m.w_hi = [sb(f"w_hi{l}", [P, C, widths[l]], F32R) for l in range(LAYERS + 1)]
        m.w_lo = [sb(f"w_lo{l}", [P, C, widths[l]], F32R) for l in range(LAYERS + 1)]
        m.brows = sb("brows", [1, 2 * D + D], F32)
        m.bo_row = sb("bo_row", [1, D], F32)
        m.bo_rest = sb("bo_rest", [1, 2, D], F32)
        m.bo_parts = sb("bo_parts", [1, 3, D], BF16)
        m.bo_3 = sb("bo_3", [3, D], BF16)
        m.bin_c = sb("bin_c", [P, C], F32)
        m.bin_b = sb("bin_b", [P, C, P], F32)
        m.bias0 = sb("bias0", [P, WIDE], F32)
        m.bias_p = [None] + [sb(f"bias_p{l}", [P, 2, D], F32) for l in (1, 2)]

        m.tgt_i = sb("tgt_i", [P, EK], I32)
        m.src_i = sb("src_i", [P, EK], I32)
        m.e_tmp = sb("e_tmp", [P, EK], I32)
        m.e_tmp2 = sb("e_tmp2", [P, EK], I32)
        m.tgt_f = sb("tgt_f", [P, EK], F32)
        m.bucket_f = sb("bucket_f", [P, EK], F32)
        m.lo_f = sb("lo_f", [P, EK], F32)
        m.num_lo_f = sb("num_lo_f", [P, EK], F32)
        m.num_hi_f = sb("num_hi_f", [P, EK], F32)
        m.slot_i = sb("slot_i", [P, NT], I32)
        m.slot_lo = sb("slot_lo", [P, NT], F32)
        m.slot_src = sb("slot_src", [P, NT], I32)
        m.inv_deg = sb("inv_deg", [P, NT], F32)
        m.full_m = sb("full_m", [P, NT], F32)
        m.tab_a = sb("tab_a", [P, NT], F32)
        m.tab_b = sb("tab_b", [P, NT], F32)
        m.flag_f = sb("flag_f", [P, 1], F32)
        m.flag_i = sb("flag_i", [P, 1], I32)

        m.in_buf = sb("in_buf", [P, 2, TPG * D], F32)
        m.x_buf = sb("x_buf", [P, 2, TPG * D], F32)
        m.p_out = sb("p_out", [P, 2, TPG * D], F32)
        m.t_raw = sb("t_raw", [P, 4, D], F32)
        m.t_out = sb("t_out", [P, 2, TPG * D], F32)
        m.hT_hi = sb("hT_hi", [P, 2, 2, C, P], F32R)
        m.hT_lo = sb("hT_lo", [P, 2, 2, C, P], F32R)
        m.gath = sb("gath", [P, 8, D], F32)
        m.gath_hi = sb("gath_hi", [P, 2, 2, D], F32R)
        m.gath_lo = sb("gath_lo", [P, 2, 2, D], F32R)
        m.idx8 = sb("idx8", [P, 2, 8], I32)
        m.pick = sb("pick", [P, 2, 2, P], F32R)
        m.v_buf = sb("v_buf", [P, 2, 2, D], F32)
        m.pick_f = sb("pick_f", [P, 8, P], F32)
        m.lo8 = sb("lo8", [P, 2, 8], F32)
        m.y_buf = sb("y_buf", [P, 8, D], F32)
        m.square = sb("square", [P, 8, D], BF16)
        m.y_sum = sb("y_sum", [P, 8], F32)
        m.minus_mean = sb("minus_mean", [P, 8], F32)
        m.squares = sb("squares", [P, 8], F32)
        m.ve = sb("ve", [P, 8], F32)
        m.eps = sb("eps", [P, 1], F32)
        m.root = sb("root", [P, 8], F32)
        m.newton = sb("newton", [P, 8], F32)
        m.rstd = sb("rstd", [P, 8], F32)
        m.shift = sb("shift", [P, 8], F32)
        m.over_src = sb("over_src", [P, 1], I32)
        m.over_row = sb("over_row", [P, 1], I32)
        m.over_spread = sb("over_spread", [P, P], F32)
        m.over_bucket = sb("over_bucket", [P, NT], F32)
        m.over_lo = sb("over_lo", [P, P], F32)
        m.over_loT = sb("over_loT", [P, P], F32)
        m.over_earlier = sb("over_earlier", [P, P], F32)
        m.over_n = sb("over_n", [P, 5], F32)
        m.over_same = sb("over_same", [P, P], F32)
        m.oh_bucket = sb("oh_bucket", [P, 2, NT], F32R)
        m.oh_lo = sb("oh_lo", [P, 2, P], F32R)
        m.at_slot = sb("at_slot", [P, 2, 2, P], F32R)
        m.rank = sb("rank", [P, 2], F32)
        m.junk = sb("junk", [P, NT], F32)

        m.ps = ctx.enter_context(nc.psum_tensor("ps", [P, 8, 512], F32))

        m.x0_in = [ctx.enter_context(nc.semaphore(f"x0_in{q}")) for q in range(2)]
        m.p_in = [[ctx.enter_context(nc.semaphore(f"p_in{l}_{q}")) for q in range(2)] for l in range(LAYERS)]
        m.N, m.NG, m.NT, m.NROW, m.LASTP = N, NG, NT, NROW, LASTP
        m.EK, m.EFULL, m.EREST, m.NI = EK, EFULL, EREST, NI
        m.x, m.src, m.dst, m.w_in, m.b_in, m.w_agg, m.w_self = x, src, dst, w_in, b_in, w_agg, w_self
        m.b_hid, m.w_out, m.b_out, m.out = b_hid, w_out, b_out, out

        prepare_constants_and_weights(nc, m)
        first_pass_and_buckets(nc, m)
        for layer in (1, 2):
            add_overfull_buckets(nc, m, layer - 1)
            middle_pass(nc, m, layer)
        add_overfull_buckets(nc, m, LAYERS - 1)
        last_pass(nc, m)


_INS = ["x", "src", "dst", "L0_gnn_W_in", "L0_gnn_b_in", "L0_gnn_W_agg", "L0_gnn_W_self", "L0_gnn_b_hid",
        "L0_gnn_W_out", "L0_gnn_b_out"]


def kernel(**inputs):
    import concourse.bacc as bacc
    from concourse.bass_utils import run_bass_kernel_spmd

    nc = bacc.Bacc("TRN2", target_bir_lowering=False, num_devices=1)
    arrays, args = {}, []
    for name in _INS:
        a = np.ascontiguousarray(inputs[name])
        arrays[f"in_{name}"] = a
        args.append(nc.dram_tensor(f"in_{name}", a.shape, mybir.dt.from_np(a.dtype), kind="ExternalInput").ap())
    out = nc.dram_tensor("out_0", inputs["x"].shape, F32, kind="ExternalOutput").ap()
    build_program(nc, *args, out)
    result = run_bass_kernel_spmd(nc, [arrays], core_ids=[0])
    return result.results[0]["out_0"]
```
